# Optimizing a Trainium2 kernel written in Bass

```python
import numpy as np
import jax
import jax.numpy as jnp

def _softmax(x, axis=-1):
    return jax.nn.softmax(x, axis=axis)

def _gelu(x):
    return jax.nn.gelu(x, approximate=True)

def _silu(x):
    return jax.nn.silu(x)

def _sigmoid(x):
    return jax.nn.sigmoid(x)

def _layernorm(x, axis=-1, eps=1e-05):
    m = jnp.mean(x, axis=axis, keepdims=True)
    v = jnp.var(x, axis=axis, keepdims=True)
    return (x - m) / jnp.sqrt(v + eps)

def _scatter_add(tgt, idx, src, axis=0):
    return tgt.at[idx].add(src)

def _segment_sum(src, seg, n):
    return jax.ops.segment_sum(src, seg, n)
kernel_name = 'mk_xattn_ffn_d1_seqx_r8_e18c1c'

def setup_inputs(seed: int=0):
    np.random.seed(seed)
    _w = jnp.asarray

    def _rec_inputs():
        import jax
        import jax.numpy as jnp
        _rk = jax.random.key(seed)
        x = -0.0005207 + 1.001 * jax.random.normal(jax.random.fold_in(_rk, 1), (8, 128, 256), jnp.float32)
        _lenS = 128 - jax.random.randint(jax.random.fold_in(_rk, 7), (8,), 0, max(1, 128 // 4) + 1, jnp.int32)
        _lenS2 = 128 - jax.random.randint(jax.random.fold_in(_rk, 8), (8,), 0, max(1, 128 // 4) + 1, jnp.int32)
        _ctx_2048P = jax.random.normal(jax.random.fold_in(_rk, 11), (8, 16, 256), jnp.float32)
        _ctx_2048c = jax.random.dirichlet(jax.random.fold_in(_rk, 511), 0.3 * jnp.ones((16,), jnp.float32), (8, 128))
        _ctx_2048t = jnp.einsum('bsk,bkd->bsd', _ctx_2048c, _ctx_2048P)
        _ctx_2048t = _ctx_2048t * jax.lax.rsqrt(jnp.mean(jnp.square(_ctx_2048t)) + 1e-12) * 0.953939
        ctx_2048 = 2.81802e-05 + 1.00001 * (_ctx_2048t + 0.3 * jax.random.normal(jax.random.fold_in(_rk, 611), (8, 128, 256), jnp.float32))
        pos_BxS2 = jnp.broadcast_to(jnp.arange(128, dtype=jnp.int32), (8, 128))
        itok_BxS_4096_4607 = jax.random.randint(jax.random.fold_in(_rk, 13), (8, 128), 512, 576, jnp.int32)
        return (x, ctx_2048, pos_BxS2, itok_BxS_4096_4607)
    x, ctx_2048, pos_BxS2, itok_BxS_4096_4607 = _rec_inputs()

    def _L0_xattn_setup():
        import jax, jax.numpy as jnp
        import numpy as np
        B, CTX, DRAFT, D = (2, 512, 64, 256)
        H, KVH, HD = (16, 4, 128)
        N_REP = H // KVH
        EPS = 1e-06
        THETA = 10000.0
        SCALE = 1.0 / np.sqrt(HD).astype(np.float32)

        def _rms_norm(x, w):
            v = jnp.mean(jnp.square(x.astype(jnp.float32)), axis=-1, keepdims=True)
            return (w * (x.astype(jnp.float32) * jax.lax.rsqrt(v + EPS))).astype(x.dtype)

        def _rotate_half(x):
            x1, x2 = jnp.split(x, 2, axis=-1)
            return jnp.concatenate((-x2, x1), axis=-1)

        def _rope(x, pos):
            inv_freq = 1.0 / THETA ** (jnp.arange(0, HD, 2, dtype=jnp.float32) / HD)
            freqs = pos.astype(jnp.float32)[:, None, :, None] * inv_freq
            emb = jnp.concatenate((freqs, freqs), axis=-1)
            return x * jnp.cos(emb) + _rotate_half(x) * jnp.sin(emb)
        key = jax.random.key(seed)
        ks = jax.random.split(key, 6)
        return {'draft_hidden': jax.random.normal(ks[0], (B, DRAFT, D), jnp.float32), 'context_hidden': jax.random.normal(ks[1], (B, CTX, D), jnp.float32), 'Wq': jax.random.normal(ks[2], (H * HD, D), jnp.float32) * 0.02, 'Wk': jax.random.normal(ks[3], (KVH * HD, D), jnp.float32) * 0.02, 'Wv': jax.random.normal(ks[4], (KVH * HD, D), jnp.float32) * 0.02, 'Wo': jax.random.normal(ks[5], (D, H * HD), jnp.float32) * 0.02, 'q_norm_w': jnp.ones((HD,), jnp.float32), 'k_norm_w': jnp.ones((HD,), jnp.float32), 'context_position_ids': jnp.broadcast_to(jnp.arange(CTX, dtype=jnp.int32), (B, CTX)), 'draft_position_ids': jnp.broadcast_to(CTX + jnp.arange(DRAFT, dtype=jnp.int32), (B, DRAFT))}
    _L0_xattn_all = _L0_xattn_setup()
    _L0_xattn_in = {k: v for k, v in _L0_xattn_all.items() if k in ('Wq', 'Wk', 'Wv', 'Wo', 'q_norm_w', 'k_norm_w')}
    del _L0_xattn_all

    def _L0_ffn_setup():
        import jax, jax.numpy as jnp
        import numpy as np
        H = 256
        E = 8
        K = 2
        I = 16
        key = jax.random.key(seed)
        k1, k2, k3, k4 = jax.random.split(key, 4)
        B, T = (2, 512)
        x = jax.random.normal(k1, (B, T, H), dtype=jnp.float32)
        router_w = jax.random.normal(k2, (E, H), dtype=jnp.float32) / np.sqrt(H)
        down_w = jax.random.normal(k3, (E, I, H), dtype=jnp.float32) / np.sqrt(H)
        up_w = jax.random.normal(k4, (E, H, I), dtype=jnp.float32) / np.sqrt(I)
        return {'x': x, 'router_w': router_w, 'down_w': down_w, 'up_w': up_w}
    _L0_ffn_all = _L0_ffn_setup()
    _L0_ffn_in = {k: v for k, v in _L0_ffn_all.items() if k in ('router_w', 'down_w', 'up_w')}
    del _L0_ffn_all
    return {'x': x, 'ctx_2048': ctx_2048, 'pos_BxS2': pos_BxS2, 'itok_BxS_4096_4607': itok_BxS_4096_4607, 'L0_xattn_Wq': _L0_xattn_in['Wq'], 'L0_xattn_Wk': _L0_xattn_in['Wk'], 'L0_xattn_Wv': _L0_xattn_in['Wv'], 'L0_xattn_Wo': _L0_xattn_in['Wo'], 'L0_xattn_q_norm_w': _L0_xattn_in['q_norm_w'], 'L0_xattn_k_norm_w': _L0_xattn_in['k_norm_w'], 'L0_ffn_router_w': _L0_ffn_in['router_w'], 'L0_ffn_down_w': _L0_ffn_in['down_w'], 'L0_ffn_up_w': _L0_ffn_in['up_w']}

def reference(x, ctx_2048, pos_BxS2, itok_BxS_4096_4607, L0_xattn_Wq, L0_xattn_Wk, L0_xattn_Wv, L0_xattn_Wo, L0_xattn_q_norm_w, L0_xattn_k_norm_w, L0_ffn_router_w, L0_ffn_down_w, L0_ffn_up_w):
    import jax
    import jax.numpy as jnp

    def _L0_xattn_ref(draft_hidden, context_hidden, Wq, Wk, Wv, Wo, q_norm_w, k_norm_w, context_position_ids, draft_position_ids):
        import jax, jax.numpy as jnp
        import numpy as np
        B, CTX, DRAFT, D = (2, 512, 64, 256)
        H, KVH, HD = (16, 4, 128)
        N_REP = H // KVH
        EPS = 1e-06
        THETA = 10000.0
        SCALE = 1.0 / np.sqrt(HD).astype(np.float32)

        def _rms_norm(x, w):
            v = jnp.mean(jnp.square(x.astype(jnp.float32)), axis=-1, keepdims=True)
            return (w * (x.astype(jnp.float32) * jax.lax.rsqrt(v + EPS))).astype(x.dtype)

        def _rotate_half(x):
            x1, x2 = jnp.split(x, 2, axis=-1)
            return jnp.concatenate((-x2, x1), axis=-1)

        def _rope(x, pos):
            inv_freq = 1.0 / THETA ** (jnp.arange(0, HD, 2, dtype=jnp.float32) / HD)
            freqs = pos.astype(jnp.float32)[:, None, :, None] * inv_freq
            emb = jnp.concatenate((freqs, freqs), axis=-1)
            return x * jnp.cos(emb) + _rotate_half(x) * jnp.sin(emb)
        bsz, draft_len, _ = draft_hidden.shape
        ctx_len = context_hidden.shape[1]
        total_len = ctx_len + draft_len
        q = (draft_hidden @ Wq.T).reshape(bsz, draft_len, H, HD)
        q = _rms_norm(q, q_norm_w).transpose(0, 2, 1, 3)
        kv_in = jnp.concatenate([context_hidden, draft_hidden], axis=1)
        k = (kv_in @ Wk.T).reshape(bsz, total_len, KVH, HD)
        v = (kv_in @ Wv.T).reshape(bsz, total_len, KVH, HD).transpose(0, 2, 1, 3)
        k = _rms_norm(k, k_norm_w).transpose(0, 2, 1, 3)
        full_position_ids = jnp.concatenate([context_position_ids, draft_position_ids], axis=1)
        q = _rope(q, draft_position_ids)
        k = _rope(k, full_position_ids)
        k = jnp.repeat(k, N_REP, axis=1)
        v = jnp.repeat(v, N_REP, axis=1)
        scores = jnp.einsum('bhqd,bhkd->bhqk', q, k) * SCALE
        probs = jax.nn.softmax(scores, axis=-1)
        attn = jnp.einsum('bhqk,bhkd->bhqd', probs, v)
        attn = attn.transpose(0, 2, 1, 3).reshape(bsz, draft_len, H * HD)
        return attn @ Wo.T

    def _L0_ffn_ref(x, router_w, down_w, up_w):
        import jax, jax.numpy as jnp
        import numpy as np
        H = 256
        E = 8
        K = 2
        I = 16
        logits = jnp.einsum('bth,eh->bte', x, router_w)
        weights = jax.nn.softmax(logits, axis=-1)
        top_w, top_idx = jax.lax.top_k(weights, K)
        topk_mask = jnp.sum(jax.nn.one_hot(top_idx, E, dtype=x.dtype), axis=-2)
        gate = weights * topk_mask
        h = jnp.einsum('bth,eih->beti', x, down_w)
        a = jax.nn.silu(h)
        expert_out = jnp.einsum('beti,ehi->beth', a, up_w)
        out = jnp.einsum('beth,bte->bth', expert_out, gate)
        return out
    x = x + _L0_xattn_ref(_layernorm(x, axis=-1), ctx_2048, L0_xattn_Wq, L0_xattn_Wk, L0_xattn_Wv, L0_xattn_Wo, L0_xattn_q_norm_w, L0_xattn_k_norm_w, pos_BxS2, itok_BxS_4096_4607)
    x = x + _L0_ffn_ref(_layernorm(x, axis=-1), L0_ffn_router_w, L0_ffn_down_w, L0_ffn_up_w)
    return x

_drawn_inputs = setup_inputs


def setup_inputs(seed=0):
    import zlib

    import numpy as np

    out = dict(_drawn_inputs(seed))
    spreads = {'L0_xattn_q_norm_w': (1.0, 0.6), 'L0_xattn_k_norm_w': (1.0, 0.6)}
    factors = {}
    for name, (base, spread) in spreads.items():
        noise = np.random.default_rng([zlib.crc32(name.encode()), seed]).standard_normal(out[name].shape)
        drawn = base * np.exp(spread * noise) if base else spread * noise
        out[name] = jnp.asarray(drawn.astype(out[name].dtype))
    for name, factor in factors.items():
        out[name] = (out[name] * factor).astype(out[name].dtype)
    return out
```

```python
import math
from contextlib import ExitStack

import concourse.bass as bass
from concourse import mybir

F32 = mybir.dt.float32
F32R = mybir.dt.float32r
I32 = mybir.dt.int32
ALU = mybir.AluOpType
ACT = mybir.ActivationFunctionType
AX = mybir.AxisListType

B, S, D = 8, 128, 256
HEADS, KV, HD = 16, 4, 128
REP = HEADS // KV
P = 128
DT = D // P
HALF = HD // 2
NE, NI = 8, 16
EI = NE * NI
GRP = REP * HD
KEYS = 2 * S
CH = DT * GRP
GROUPS = B * KV
RMS_EPS, LN_EPS = 1e-6, 1e-5

PAIR = 2 * KV
LOOP_FROM = PAIR + 1
LOOP_TO = GROUPS - PAIR + 1
TAIL_TO = GROUPS + KV + 1

MAGIC = 1.5 * 2.0 ** 23
TWO_PI = (6.28125, 0.0019350051879882812, 3.019916050561733e-07)
PI_F32 = 3.1415925


def after(engine, sem, count):
    if not (isinstance(count, int) and count <= 0):
        engine.wait_ge(sem, count)


def xattn_ffn(nc, x_d, ctxT_d, pos_d, w_d, norm_d, ffn_in_d, up_d, freq_d, out_d):
    x_rows = x_d.rearrange("b s d -> (b s) d")
    ctx_rows = ctxT_d.rearrange("b p n -> (b p) n")
    out_rows = out_d.rearrange("b s d -> (b s) d")

    with ExitStack() as ctx:
        def sb(name, shape, dt=F32):
            return ctx.enter_context(nc.sbuf_tensor(name, shape, dt))

        def sem(name):
            return ctx.enter_context(nc.semaphore(name))

        ident = sb("ident", [P, P])
        neg_half = sb("neg_half", [P, 8])
        earlier = sb("earlier", [P, NE, NE])
        ln_eps = sb("ln_eps", [P, 1])
        rms_eps = sb("rms_eps", [P, REP])
        half_pi = sb("half_pi", [P, 1])
        wK, wV, wQ, wO = 0, 1, 2, 6
        w_order = [wK, wQ, wV, wQ + 1, wQ + 2, wO, wQ + 3, wO + 1, wO + 2, wO + 3]
        RAW = 5
        w_raw = sb("w_raw", [P, RAW, CH])
        w_hi = sb("w_hi", [P, 10, CH], F32R)
        w_lo = sb("w_lo", [P, 10, CH], F32R)
        ffn_in_w = sb("ffn_in_w", [P, DT, NE + EI])
        up_w = sb("up_w", [P, D])
        norm_w = sb("norm_w", [P, 2, 2, HALF])
        norm_sw = sb("norm_sw", [P, 2, 2, HALF])
        freq = sb("freq", [P, HALF])
        pos_i = sb("pos_i", [P, 2 * B], I32)
        pos_f = sb("pos_f", [P, 2 * B])
        cos_t = sb("cos_t", [P, 2 * B * HALF])
        sin_t = sb("sin_t", [P, 2 * B * HALF])
        q_tab = [sb(f"q_tab{i}", [P, 2, 2, HALF]) for i in range(2)]
        k_tab = [sb(f"k_tab{i}", [P, 2, 2, 2, HALF]) for i in range(2)]
        x_ln = sb("x_ln", [P, D])
        x_res = sb("x_res", [P, D])
        x2 = sb("x2", [P, D])
        x_out = sb("x_out", [P, D])
        bn6 = sb("bn6", [P, 2, 6])
        mv = sb("mv", [P, 2, 2])
        ve = sb("ve", [P, 2])
        rstd = sb("rstd", [P, 2])
        xn = sb("xn", [P, D])
        xn2 = sb("xn2", [P, D])
        xT_hi = [sb(f"xT_hi{i}", [P, DT, P], F32R) for i in range(2)]
        xT_lo = [sb(f"xT_lo{i}", [P, DT, P], F32R) for i in range(2)]
        ctx_raw = sb("ctx_raw", [P, DT, P])
        cT_hi = sb("cT_hi", [P, DT, P], F32R)
        cT_lo = sb("cT_lo", [P, DT, P], F32R)
        kcos = sb("kcos", [P, KV, HD])
        ksin = sb("ksin", [P, KV, HD])
        krot = sb("krot", [P, KV, HD])
        krot_n = sb("krot_n", [P, KV, HD])
        kss = sb("kss", [P, KV])
        kve = sb("kve", [P, KV])
        krs = sb("krs", [P, KV])
        kT_hi = [sb(f"kT_hi{i}", [P, KV, KEYS], F32R) for i in range(2)]
        kT_lo = [sb(f"kT_lo{i}", [P, KV, KEYS], F32R) for i in range(2)]
        v_hi = [sb(f"v_hi{i}", [P, 2, KV * HD], F32R) for i in range(2)]
        v_lo = [sb(f"v_lo{i}", [P, 2, KV * HD], F32R) for i in range(2)]
        qprod = sb("qprod", [P, 2, REP, HD])
        qcos, qsin = qprod[:, 0], qprod[:, 1]
        qrot = sb("qrot", [P, REP, HD])
        qss = sb("qss", [P, REP])
        qve = sb("qve", [P, REP])
        qscale = sb("qscale", [P, REP])
        qT_hi = sb("qT_hi", [P, REP, P], F32R)
        qT_lo = sb("qT_lo", [P, REP, P], F32R)
        smax = sb("smax", [P, REP])
        sbias = sb("sbias", [P, REP])
        probs = sb("probs", [P, REP, KEYS])
        turns = qprod[:, :, :, :].rearrange("p k h d -> p (k h d)")
        ang = probs[:, :, :].rearrange("p h n -> p (h n)")
        psums = sb("psums", [P, REP])
        rsums = sb("rsums", [P, REP])
        pT_hi = sb("pT_hi", [P, 2, REP * P], F32R)
        pT_lo = sb("pT_lo", [P, 2, REP * P], F32R)
        aT_hi = sb("aT_hi", [P, REP, P], F32R)
        aT_lo = sb("aT_lo", [P, REP, P], F32R)
        x2T = sb("x2T", [P, DT, P])
        lmax = sb("lmax", [P, 1])
        lexp = sb("lexp", [P, NE])
        lsum = sb("lsum", [P, 1])
        lrec = sb("lrec", [P, 1])
        htanh = sb("htanh", [P, NE, NI])
        beats = sb("beats", [P, NE, NE])
        ties = sb("ties", [P, NE, NE])
        rank = sb("rank", [P, NE])
        gate = sb("gate", [P, NE])
        gate_n = sb("gate_n", [P, NE])
        silu2 = sb("silu2", [P, NE, NI])
        act_g = sb("act_g", [P, NE, NI])
        agT = sb("agT", [P, P])

        def bank(name):
            return ctx.enter_context(nc.psum_tensor(name, [P, 512], F32))
        ps_q = bank("ps_q")
        ps_kv = bank("ps_kv")
        ps_tr = bank("ps_tr")
        ps_s = [bank("ps_s0"), bank("ps_s1")]
        ps_pT = [bank("ps_pT0"), bank("ps_pT1")]
        ps_att = ps_pT[1]
        ps_o = bank("ps_o")

        s_pos, s_small, s_xln, s_ctx, s_xres, s_store = (
            sem(n) for n in ("pos_loaded", "small_loaded", "xln_loaded", "ctx_loaded", "xres_loaded", "out_stored"))
        s_w = [sem(f"w_loaded{i}") for i in range(10)]
        s_norm = sem("norm_weights_loaded")
        s_const = sem("constants_made")
        s_whi, s_wlo_dve, s_wlo_pool = sem("w_hi_made"), sem("w_lo_dve"), sem("w_lo_pool")
        s_posf, s_ang, s_abs, s_trig = sem("pos_float"), sem("angles_made"), sem("abs_made"), sem("trig_made")
        s_dve = sem("dve_chain")
        s_pool = sem("pool_chain")
        s_qtab, s_ktab = sem("q_tables_made"), sem("k_tables_made")
        s_bn, s_mv, s_rstd, s_xn = sem("ln_stats"), sem("ln_mean_var"), sem("ln_rstd"), sem("ln_done")
        s_ve = sem("ln_var_eps")
        s_bn2, s_mv2, s_rstd2, s_xn2 = sem("ln2_stats"), sem("ln2_mean_var"), sem("ln2_rstd"), sem("ln2_done")
        s_ve2 = sem("ln2_var_eps")
        s_xTps, s_xThi, s_xTlo = sem("xT_in_psum"), sem("xT_hi_made"), sem("xT_lo_made")
        s_chi, s_clo = sem("ctx_hi_made"), sem("ctx_lo_made")
        s_kvps, s_kprod, s_ksq = sem("kv_in_psum"), sem("k_products"), sem("k_squares")
        s_kadd, s_kve, s_krs, s_kn = sem("k_rotated"), sem("k_var_eps"), sem("k_rstd"), sem("k_normed")
        s_kTps, s_kThi, s_kTlo = sem("kT_in_psum"), sem("kT_hi_made"), sem("kT_lo_made")
        s_vhi, s_vlo = sem("v_hi_made"), sem("v_lo_made")
        s_qps, s_qprod, s_qsq = sem("q_in_psum"), sem("q_products"), sem("q_squares")
        s_qrot, s_qve, s_qscale = sem("q_rotated"), sem("q_var_eps"), sem("q_scale_made")
        s_qTps, s_qThi, s_qTlo = sem("qT_in_psum"), sem("qT_hi_made"), sem("qT_lo_made")
        s_score = [sem("scores0"), sem("scores1")]
        s_max, s_bias = sem("score_max"), sem("score_bias")
        s_exp = [sem("exp0"), sem("exp1")]
        s_rec, s_pn_pool, s_pn_dve = sem("sum_reciprocals"), sem("probs_scaled_pool"), sem("probs_scaled_dve")
        s_pTps = [sem("pT_in_psum0"), sem("pT_in_psum1")]
        s_pThi = [sem("pT_hi0"), sem("pT_hi1")]
        s_pTlo = [sem("pT_lo0"), sem("pT_lo1")]
        s_att, s_ahi, s_alo = sem("att_in_psum"), sem("att_hi_made"), sem("att_lo_made")
        s_wo = sem("projected")
        s_x2 = sem("residual_added")
        s_x2Tps, s_x2T = sem("x2T_in_psum"), sem("x2T_made")
        s_h, s_lmax, s_lact, s_gate = sem("h_in_psum"), sem("logit_max"), sem("ffn_activated"), sem("ffn_gated")
        s_f = sem("ffn_chain")
        s_agTps, s_agT = sem("agT_in_psum"), sem("agT_made")
        s_y, s_out = sem("y_in_psum"), sem("out_made")

        def raw(c):
            return w_raw[:, w_order.index(c) % RAW, :]

        def flags(n):
            s, b = n % KV, n // KV
            return s, b, b % 2

        def run_slots(engine, slot):
            for n in range(LOOP_FROM):
                slot(n, n)
            with engine.Fori(0, (LOOP_TO - LOOP_FROM) // PAIR) as turn:
                first = engine.snap(turn * PAIR + LOOP_FROM)
                for i in range(PAIR):
                    slot(first + i, LOOP_FROM + i)
            for n in range(LOOP_TO, TAIL_TO):
                slot(n, n)

        block = ctx.enter_context(nc.Block())

        @block.sync
        def _(sp):
            def load_ctx(r, first=False):
                sp.dma_start(ctx_raw[:, :, :], ctx_rows[r, :].rearrange("p (t n) -> p t n", t=DT)).then_inc(s_ctx, 16)

            def load_w(c):
                sp.dma_start(raw(c), w_d[c]).then_inc(s_w[c], 16)

            sp.dma_start(pos_i[:, :], pos_d).then_inc(s_pos, 16)
            sp.dma_start(freq[:, :], freq_d.partition_broadcast(P)).then_inc(s_pos, 16)
            sp.dma_start(x_ln[:, :], x_rows[0:P, :]).then_inc(s_xln, 16)
            load_ctx(slice(0, P))
            for c in w_order[:3]:
                load_w(c)
            sp.dma_start(norm_w[:, :, :, :].rearrange("p a h f -> p (a h f)"),
                         norm_d.partition_broadcast(P)).then_inc(s_norm, 16)
            for c in w_order[3:RAW]:
                load_w(c)
            sp.dma_start(ffn_in_w[:, :, :], ffn_in_d).then_inc(s_small, 16)
            sp.dma_start(up_w[:, :], up_d).then_inc(s_small, 16)
            sp.wait_ge(s_xn, KV)
            sp.dma_start(x_ln[:, :], x_rows[P:2 * P, :]).then_inc(s_xln, 16)
            sp.wait_ge(s_chi, KV)
            sp.wait_ge(s_clo, KV)
            load_ctx(slice(P, 2 * P))

            split_by = (s_wlo_pool, s_wlo_dve, s_wlo_pool, s_wlo_dve, s_wlo_dve)
            for c, split, count in zip(w_order[RAW:], split_by, (1, 1, 2, 2, 3)):
                sp.wait_ge(split, count)
                load_w(c)

            def step(g, b):
                row = g * (P // KV)

                def rows(ahead):
                    at = row + ahead * P
                    return slice(at, at + P) if isinstance(at, int) else bass.ds(at, P)
                if b + 2 < B:
                    sp.wait_ge(s_xn, g + 2 * KV)
                    sp.dma_start(x_ln[:, :], x_rows[rows(2), :]).then_inc(s_xln, 16)
                if b < B:
                    after(sp, s_x2, g)
                    sp.dma_start(x_res[:, :], x_rows[rows(0), :]).then_inc(s_xres, 16)
                if b + 2 < B:
                    sp.wait_ge(s_chi, g + 2 * KV)
                    sp.wait_ge(s_clo, g + 2 * KV)
                    load_ctx(rows(2))
                if b >= 2:
                    sp.wait_ge(s_out, g - KV)
                    sp.dma_start(out_rows[rows(-2), :], x_out[:, :]).then_inc(s_store, 16)

            for b in range(2):
                step(KV * b, b)
            with sp.Fori(0, B - 4) as turn:
                step(sp.snap(turn * KV + 2 * KV), 2)
            for b in range(B - 2, B + 2):
                step(KV * b, b)
            sp.wait_ge(s_store, 16 * B)

        @block.gpsimd
        def _(pool):
            g_ = nc.gpsimd
            count = [0]

            def link(ins):
                count[0] += 1
                ins.then_inc(s_pool, 1)
                pool.wait_ge(s_pool, count[0])

            g_.memset(neg_half[:, :], -0.5).then_inc(s_const, 1)
            g_.memset(ln_eps[:, :], LN_EPS)
            g_.memset(rms_eps[:, :], HD * RMS_EPS)
            g_.memset(half_pi[:, :], math.pi / 2).then_inc(s_const, 1)
            link(g_.memset(ident[:, :], 0.0))
            g_.affine_select(out=ident[:, :], in_=ident[:, :], compare_op=ALU.not_equal, fill=1.0, base=0,
                             pattern=[[-1, P]], channel_multiplier=1).then_inc(s_const, 1)
            link(g_.memset(earlier[:, :, :], 1.0))
            g_.affine_select(out=earlier[:, :, :], in_=earlier[:, :, :], compare_op=ALU.is_gt, fill=0.0, base=0,
                             pattern=[[1, NE], [-1, NE]], channel_multiplier=0).then_inc(s_const, 1)
            pool.wait_ge(s_const, 4)

            def ctx_lo(b16, b4):
                after(pool, s_ctx, b16)
                after(pool, s_chi, b4)
                g_.tensor_tensor(cT_lo[:, :, :], ctx_raw[:, :, :], cT_hi[:, :, :].bitcast(F32),
                                 ALU.subtract).then_inc(s_clo, KV)

            def w_lo_pool(c, n):
                pool.wait_ge(s_whi, n)
                g_.tensor_tensor(w_lo[:, c, :], raw(c), w_hi[:, c, :].bitcast(F32),
                                 ALU.subtract).then_inc(s_wlo_pool, 1)

            def tables(g, tile, dst, which, done, inc):
                at = g * (2 * HALF // KV) + tile * HALF
                cols = slice(at, at + HALF) if isinstance(at, int) else bass.ds(at, HALF)
                for kind, t, w in ((0, cos_t, norm_w), (1, sin_t, norm_sw)):
                    src = t[:, cols].unsqueeze(1).to_broadcast([P, 2, HALF])
                    g_.tensor_tensor(dst[:, kind, :, :], w[:, which, :, :], src, ALU.mult).then_inc(done, inc)

            def q_tables(g, p):
                tables(g, 1, q_tab[p], 0, s_qtab, KV // 2)

            def k_tables(g, p):
                for tile in range(2):
                    tables(g, tile, k_tab[p][:, tile], 1, s_ktab, KV // 4)

            def rsqrt(var, src, dst, done_add, done, eps, cols, n_add, step):
                g_.tensor_tensor(var, src, eps[:, 0:cols], ALU.add).then_inc(done_add, step)
                pool.wait_ge(done_add, n_add)
                g_.tensor_tensor(dst, var, neg_half[:, 0:cols], ALU.pow).then_inc(done, step)

            def ln1(g):
                pool.wait_ge(s_mv, g + KV)
                rsqrt(ve[:, 0:1], mv[:, 0, 1:2], rstd[:, 0:1], s_ve, s_rstd, ln_eps, 1, g + KV, KV)

            def rotate(out, c, s_):
                g_.tensor_tensor(out[:, :, 0:HALF], c[:, :, 0:HALF], s_[:, :, HALF:HD], ALU.add)
                return g_.tensor_tensor(out[:, :, HALF:HD], c[:, :, HALF:HD], s_[:, :, 0:HALF], ALU.add)

            def q_add(g):
                pool.wait_ge(s_qprod, g + 1)
                rotate(qrot, qcos, qsin).then_inc(s_qrot, 1)

            def q_scale(g):
                pool.wait_ge(s_qsq, g + 1)
                rsqrt(qve[:, :], qss[:, :], qscale[:, :], s_qve, s_qscale, rms_eps, REP, g + 1, 1)

            def k_unit(u):
                half = 2
                pool.wait_ge(s_kprod, u)
                rotate(krot, kcos, ksin).then_inc(s_kadd, half)
                pool.wait_ge(s_ksq, u)
                rsqrt(kve[:, :], kss[:, :], krs[:, :], s_kve, s_krs, rms_eps, KV, u, half)
                pool.wait_ge(s_kadd, u)
                pool.wait_ge(s_krs, u)
                g_.tensor_tensor(krot_n[:, :, :], krot[:, :, :],
                                 krs[:, :].unsqueeze(2).to_broadcast([P, KV, HD]), ALU.mult).then_inc(s_kn, half)

            def scale_probs(g):
                pool.wait_ge(s_rec, g + 1)
                g_.tensor_tensor(probs[:, 0:2, :], probs[:, 0:2, :],
                                 rsums[:, 0:2].unsqueeze(2).to_broadcast([P, 2, KEYS]), ALU.mult).then_inc(s_pn_pool, 1)

            ctx_lo(16, KV)
            w_lo_pool(wK, 1)
            ln1(0)
            w_lo_pool(wV, 3)
            pool.wait_ge(s_norm, 16)
            link(g_.tensor_scalar(norm_w[:, 1, :, :], norm_w[:, 1, :, :], math.sqrt(HD), 1.0, ALU.mult, ALU.mult))
            link(g_.tensor_scalar(norm_sw[:, :, 0, :], norm_w[:, :, 0, :], 1.0, 1.0, ALU.mult, ALU.mult))
            link(g_.tensor_scalar(norm_sw[:, :, 1, :], norm_w[:, :, 1, :], -1.0, 1.0, ALU.mult, ALU.mult))
            pool.wait_ge(s_trig, 2)
            k_tables(0, 0)
            q_tables(0, 0)
            k_unit(2)
            q_add(0)
            pool.wait_ge(s_kTps, 2)
            k_unit(4)
            q_scale(0)
            pool.wait_ge(s_kvps, 3)
            ctx_lo(32, 2 * KV)
            k_tables(KV, 1)

            def slot(g, n):
                s, b, p = flags(n)
                if n + 1 < GROUPS:
                    q_add(g + 1)
                if n < GROUPS:
                    scale_probs(g)
                if s == 0 and b + 1 < B:
                    ln1(g + KV)
                if s == 1 and 1 <= b <= B:
                    pool.wait_ge(s_mv2, g - s)
                    rsqrt(ve[:, 1:2], mv[:, 1, 1:2], rstd[:, 1:2], s_ve2, s_rstd2, ln_eps, 1, g - s, KV)
                if n + 1 < GROUPS:
                    q_scale(g + 1)
                if s < 2 and b + 1 < B:
                    k_unit(g - s + KV + 2 * (s + 1))
                if s == 2 and b + 1 < B:
                    q_tables(g - s + KV, 1 - p)
                if s == 2 and b + 2 < B:
                    k_tables(g - s + 2 * KV, p)
                if s == 3 and b + 2 < B:
                    pool.wait_ge(s_kvps, g - s + KV + 3)
                    ctx_lo((g - s + 3 * KV) * 4, g - s + 3 * KV)

            run_slots(pool, slot)

        @block.scalar
        def _(act):
            a_ = nc.scalar

            def copy(dst, src):
                return a_.activation(dst, src, ACT.Copy)

            def split_w(c):
                act.wait_ge(s_w[c], 16)
                copy(w_hi[:, c, :], raw(c)).then_inc(s_whi, 1)

            def ctx_hi(b16):
                act.wait_ge(s_ctx, b16)
                copy(cT_hi[:, :, :], ctx_raw[:, :, :]).then_inc(s_chi, KV)

            def x_hi(g, p):
                act.wait_ge(s_xTps, g + KV)
                copy(xT_hi[p][:, :, :].rearrange("p t n -> p (t n)"), ps_tr[:, 0:D]).then_inc(s_xThi, KV)

            def squares(ps, ss, done, inc):
                for h in range(REP):
                    head = ps[:, h * HD:(h + 1) * HD]
                    ins = a_.activation(head, head, ACT.Square,
                                        accum_out=ss[:, h:h + 1])
                ins.then_inc(done, inc)

            def q_squares(g):
                act.wait_ge(s_qprod, g + 1)
                squares(ps_q, qss, s_qsq, 1)

            def k_squares(u):
                act.wait_ge(s_kprod, u)
                squares(ps_kv, kss, s_ksq, 2)

            def v_high(g, p, tile):
                act.wait_ge(s_kvps, g + 3 + tile)
                copy(v_hi[p][:, tile, :], ps_kv[:, :]).then_inc(s_vhi, 2)

            def k_high(u, p, tile):
                act.wait_ge(s_kTps, u)
                copy(kT_hi[p][:, :, tile * S:(tile + 1) * S],
                     ps_tr[:, :].rearrange("p (h n) -> p h n", h=KV)).then_inc(s_kThi, 2)

            def q_high(g):
                act.wait_ge(s_qTps, g + 1)
                copy(qT_hi[:, :, :].rearrange("p h n -> p (h n)"), ps_tr[:, :]).then_inc(s_qThi, 1)

            ctx_hi(16)
            split_w(wK)
            act.wait_ge(s_ang, 1)
            a_.activation(sin_t[:, :], ang[:, :], ACT.Sin).then_inc(s_trig, 1)
            a_.activation(turns[:, :], ang[:, :], ACT.Abs).then_inc(s_abs, 1)
            act.wait_ge(s_abs, 1)
            act.wait_ge(s_const, 4)
            a_.activation(cos_t[:, :], turns[:, :], ACT.Sin, bias=half_pi[:, 0:1],
                          scale=-1.0).then_inc(s_trig, 1)
            x_hi(0, 0)
            split_w(wQ)
            split_w(wV)
            k_squares(2)
            q_squares(0)
            act.wait_ge(s_kve, 2)
            k_squares(4)
            v_high(0, 0, 0)
            k_high(2, 0, 0)
            v_high(0, 0, 1)
            k_high(4, 0, 1)
            q_high(0)
            split_w(wQ + 1)
            act.wait_ge(s_kvps, 3)
            ctx_hi(32)

            def slot(g, n):
                s, b, p = flags(n)
                if 1 <= n <= GROUPS:
                    for t in range(2):
                        act.wait_ge(s_pTps[t], g)
                        copy(pT_hi[:, t, :], ps_pT[t][:, :]).then_inc(s_pThi[t], 1)
                if s == 3 and 1 <= b <= B:
                    act.wait_ge(s_lmax, g - s)
                    a_.activation(lexp[:, :], ps_kv[:, 0:NE], ACT.Exp, bias=lmax[:, 0:1], accum_out=lsum[:, 0:1])
                    a_.activation(htanh[:, :, :].rearrange("p e i -> p (e i)"), ps_kv[:, NE:NE + EI], ACT.Tanh,
                                  scale=0.5).then_inc(s_lact, KV)
                if n < GROUPS:
                    act.wait_ge(s_bias, g + 1)
                    for h in range(REP):
                        ins = a_.activation(probs[:, h, :], ps_s[h // 2][:, (h % 2) * KEYS:(h % 2 + 1) * KEYS],
                                            ACT.Exp, bias=sbias[:, h:h + 1], scale=qscale[:, h:h + 1],
                                            accum_out=psums[:, h:h + 1])
                        if h % 2:
                            ins.then_inc(s_exp[h // 2], 1)
                if n == 0:
                    split_w(wQ + 2)
                    split_w(wO)
                if n == 1:
                    split_w(wQ + 3)
                    split_w(wO + 1)
                if n in (2, 3):
                    split_w(wO + n)
                if 1 <= n <= GROUPS:
                    act.wait_ge(s_att, g)
                    copy(aT_hi[:, :, :].rearrange("p h n -> p (h n)"), ps_att[:, :]).then_inc(s_ahi, 1)
                if s in (1, 2) and b + 1 < B:
                    k_high(g - s + KV + 2 * s, 1 - p, s - 1)
                if n + 1 < GROUPS:
                    q_squares(g + 1)
                if s < 2 and b + 1 < B:
                    k_squares(g - s + KV + 2 * (s + 1))
                if s >= 2 and b + 1 < B:
                    v_high(g - s + KV, 1 - p, s - 2)
                if n + 1 < GROUPS:
                    q_high(g + 1)
                if s == 0 and b + 1 < B:
                    x_hi(g + KV, 1 - p)
                if s == 1 and 1 <= b <= B:
                    act.wait_ge(s_x2Tps, g - s)
                    copy(x2T[:, :, :].rearrange("p t n -> p (t n)"), ps_tr[:, 0:D]).then_inc(s_x2T, KV)
                if s == 3 and 1 <= b <= B:
                    act.wait_ge(s_agTps, g - s)
                    copy(agT[:, :], ps_tr[:, 0:P]).then_inc(s_agT, KV)
                if s == 3 and b + 2 < B:
                    act.wait_ge(s_kvps, g - s + KV + 3)
                    ctx_hi((g - s + 3 * KV) * 4)

            run_slots(act, slot)

        @block.vector
        def _(dve):
            v_ = nc.vector
            count = [0]

            def link(ins):
                count[0] += 1
                ins.then_inc(s_dve, 1)
                dve.wait_ge(s_dve, count[0])

            def low(dst, src, hi):
                return v_.tensor_tensor(dst, src, hi.bitcast(F32), ALU.subtract)

            def split_w(c, n):
                dve.wait_ge(s_whi, n)
                low(w_lo[:, c, :], raw(c), w_hi[:, c, :]).then_inc(s_wlo_dve, 1)

            def ln1(g):
                dve.wait_ge(s_xln, (g + KV) * 4)
                v_.bn_stats(bn6[:, 0, :], x_ln[:, :]).then_inc(s_bn, KV)

            def ln1_moments(g):
                v_.bn_aggr(mv[:, 0, :], bn6[:, 0, :]).then_inc(s_mv, KV)

            def ln1_apply(g):
                dve.wait_ge(s_rstd, g + KV)
                v_.tensor_scalar(xn[:, :], x_ln[:, :], mv[:, 0, 0:1], rstd[:, 0:1],
                                 ALU.subtract, ALU.mult).then_inc(s_xn, KV)

            def x_low(g, p):
                dve.wait_ge(s_xThi, g + KV)
                low(xT_lo[p][:, :, :].rearrange("p t n -> p (t n)"), ps_tr[:, 0:D],
                    xT_hi[p][:, :, :].rearrange("p t n -> p (t n)")).then_inc(s_xTlo, KV)

            def products(ps, tab, c, s_):
                src = ps[:, :].rearrange("p (h d) -> p h d", h=REP)
                for kind, dst in ((0, c), (1, s_)):
                    t = tab[:, kind, :, :].rearrange("p a f -> p (a f)").unsqueeze(1).to_broadcast([P, REP, HD])
                    ins = v_.tensor_tensor(dst[:, :, :], src, t, ALU.mult)
                return ins

            def q_products(g, p):
                dve.wait_ge(s_qps, g + 1)
                products(ps_q, q_tab[p], qcos, qsin).then_inc(s_qprod, 1)

            def k_products(g, p, tile):
                dve.wait_ge(s_kvps, g + 1 + tile)
                products(ps_kv, k_tab[p][:, tile], kcos, ksin).then_inc(s_kprod, 2)

            def v_low(g, p, tile):
                dve.wait_ge(s_vhi, g + 2 * (tile + 1))
                low(v_lo[p][:, tile, :], ps_kv[:, :], v_hi[p][:, tile, :]).then_inc(s_vlo, 2)

            def k_low(u, p, tile):
                dve.wait_ge(s_kThi, u)
                low(kT_lo[p][:, :, tile * S:(tile + 1) * S], ps_tr[:, :].rearrange("p (h n) -> p h n", h=KV),
                    kT_hi[p][:, :, tile * S:(tile + 1) * S]).then_inc(s_kTlo, 2)

            def q_low(g):
                dve.wait_ge(s_qThi, g + 1)
                low(qT_lo[:, :, :].rearrange("p h n -> p (h n)"), ps_tr[:, :],
                    qT_hi[:, :, :].rearrange("p h n -> p (h n)")).then_inc(s_qTlo, 1)

            dve.wait_ge(s_pos, 32)
            link(v_.tensor_copy(pos_f[:, :], pos_i[:, :]))
            link(v_.tensor_tensor(ang[:, :].rearrange("p (t f) -> p t f", f=HALF), pos_f[:, :].unsqueeze(2).to_broadcast([P, 2 * B, HALF]),
                                  freq[:, :].unsqueeze(1).to_broadcast([P, 2 * B, HALF]), ALU.mult))
            ln1(0)
            dve.wait_ge(s_bn, KV)
            ln1_moments(0)
            link(v_.tensor_scalar(turns[:, :], ang[:, :], 1.0 / (2 * math.pi), MAGIC, ALU.mult, ALU.add))
            link(v_.tensor_scalar(turns[:, :], turns[:, :], MAGIC, None, ALU.subtract))
            for part in TWO_PI:
                link(v_.scalar_tensor_tensor(ang[:, :], turns[:, :], -part, ang[:, :], ALU.mult, ALU.add))
            v_.tensor_scalar(ang[:, :], ang[:, :], PI_F32, -PI_F32, ALU.min, ALU.max).then_inc(s_ang, 1)
            ln1_apply(0)
            x_low(0, 0)
            split_w(wQ, 2)
            dve.wait_ge(s_ktab, KV)
            dve.wait_ge(s_qtab, KV)
            k_products(0, 0, 0)
            q_products(0, 0)
            dve.wait_ge(s_kadd, 2)
            k_products(0, 0, 1)
            v_low(0, 0, 0)
            k_low(2, 0, 0)
            v_low(0, 0, 1)
            k_low(4, 0, 1)
            q_low(0)
            split_w(wQ + 1, 4)

            def slot(g, n):
                s, b, p = flags(n)
                if 1 <= n <= GROUPS:
                    for t in range(2):
                        if s == 1 and t == 1 and b > 0:
                            dve.wait_ge(s_bn2, g - s)
                        dve.wait_ge(s_pThi[t], g)
                        low(pT_lo[:, t, :], ps_pT[t][:, :], pT_hi[:, t, :]).then_inc(s_pTlo[t], 1)
                if s == 1 and 1 <= b <= B:
                    if n > GROUPS:
                        dve.wait_ge(s_bn2, g - s)
                    v_.bn_aggr(mv[:, 1, :], bn6[:, 1, :]).then_inc(s_mv2, KV)
                if s == 3 and 1 <= b <= B:
                    dve.wait_ge(s_h, g - s)
                    v_.tensor_reduce(lmax[:, 0:1], ps_kv[:, 0:NE], AX.X, ALU.max, negate=True).then_inc(s_lmax, KV)
                if n < GROUPS:
                    for t in range(2):
                        dve.wait_ge(s_score[t], g + 1)
                        ins = v_.tensor_reduce(smax[:, 2 * t:2 * t + 2],
                                               ps_s[t][:, :].rearrange("p (h n) -> p h n", h=2),
                                               AX.X, ALU.max, negate=True)
                    ins.then_inc(s_max, 1)
                    dve.wait_ge(s_qscale, g + 1)
                    dve.wait_ge(s_max, g + 1)
                    v_.tensor_tensor(sbias[:, :], smax[:, :], qscale[:, :], ALU.mult).then_inc(s_bias, 1)
                if s == 0 and b + 1 < B:
                    ln1(g + KV)
                if n + 1 < GROUPS:
                    if s == 3:
                        dve.wait_ge(s_qtab, g - s + 2 * KV)
                    if s == 0 and b + 1 < B:
                        dve.wait_ge(s_bn, g + 2 * KV)
                    q_products(g + 1, p if s < 3 else 1 - p)
                if s == 0 and b + 1 < B:
                    ln1_moments(g + KV)
                if s == 3 and 1 <= b <= B:
                    experts(g - s)
                if n == 0:
                    split_w(wQ + 2, 5)
                    split_w(wO, 6)
                if n == 1:
                    split_w(wQ + 3, 7)
                    split_w(wO + 1, 8)
                if n in (2, 3):
                    split_w(wO + n, 7 + n)
                if n < GROUPS:
                    dve.wait_ge(s_exp[1], g + 1)
                    dve.wait_ge(s_exp[0], g + 1)
                    v_.reciprocal(rsums[:, :], psums[:, :]).then_inc(s_rec, 1)
                    dve.wait_ge(s_rec, g + 1)
                    for h in range(2, REP):
                        ins = v_.tensor_scalar(probs[:, h, :], probs[:, h, :], rsums[:, h:h + 1], None, ALU.mult)
                    ins.then_inc(s_pn_dve, 1)
                if 1 <= n <= GROUPS:
                    dve.wait_ge(s_ahi, g)
                    low(aT_lo[:, :, :].rearrange("p h n -> p (h n)"), ps_att[:, :],
                        aT_hi[:, :, :].rearrange("p h n -> p (h n)")).then_inc(s_alo, 1)
                if s in (1, 2) and b + 1 < B:
                    k_low(g - s + KV + 2 * s, 1 - p, s - 1)
                if s < 2 and b + 1 < B:
                    if s == 0:
                        dve.wait_ge(s_ktab, g + 2 * KV)
                    k_products(g - s + KV, 1 - p, s)
                if s >= 2 and b + 1 < B:
                    v_low(g - s + KV, 1 - p, s - 2)
                if s == 0 and b + 1 < B:
                    ln1_apply(g + KV)
                if s == 1 and 1 <= b <= B:
                    dve.wait_ge(s_rstd2, g - s)
                    v_.tensor_scalar(xn2[:, :], x2[:, :], mv[:, 1, 0:1], rstd[:, 1:2],
                                     ALU.subtract, ALU.mult).then_inc(s_xn2, KV)
                if n + 1 < GROUPS:
                    q_low(g + 1)
                if s == 0 and b + 1 < B:
                    x_low(g + KV, 1 - p)
                if s == 0 and 2 <= b <= B + 1:
                    dve.wait_ge(s_y, g - KV)
                    if b > 2:
                        dve.wait_ge(s_store, (g - 2 * KV) * 4)
                    v_.tensor_tensor(x_out[:, :], ps_kv[:, 0:D], x2[:, :], ALU.add).then_inc(s_out, KV)
                if s == 0 and 1 <= b <= B:
                    dve.wait_ge(s_xres, g * 4)
                    dve.wait_ge(s_wo, g)
                    if b > 1:
                        dve.wait_ge(s_out, g - KV)
                    v_.tensor_tensor(x2[:, :], ps_o[:, 0:D], x_res[:, :], ALU.add).then_inc(s_x2, KV)
                    dve.wait_ge(s_x2, g)
                    v_.bn_stats(bn6[:, 1, :], x2[:, :]).then_inc(s_bn2, KV)

            def experts(g):
                counted = [0]

                def then(ins, inc=1):
                    counted[0] += inc
                    ins.then_inc(s_f, inc)
                    dve.wait_ge(s_f, (g - KV) * 2 + counted[0])

                dve.wait_ge(s_lact, g)
                mine = lexp[:, :].unsqueeze(2).to_broadcast([P, NE, NE])
                other = lexp[:, :].unsqueeze(1).to_broadcast([P, NE, NE])
                v_.tensor_tensor(beats[:, :, :], other, mine, ALU.is_gt)
                then(v_.tensor_tensor(ties[:, :, :], other, mine, ALU.is_equal))
                v_.reciprocal(lrec[:, :], lsum[:, :])
                then(v_.tensor_tensor(ties[:, :, :], ties[:, :, :], earlier[:, :, :], ALU.mult))
                v_.scalar_tensor_tensor(silu2[:, :, :].rearrange("p e i -> p (e i)"),
                                        htanh[:, :, :].rearrange("p e i -> p (e i)"), 1.0,
                                        ps_kv[:, NE:NE + EI], ALU.add, ALU.mult)
                then(v_.tensor_tensor(beats[:, :, :], beats[:, :, :], ties[:, :, :], ALU.add))
                then(v_.tensor_reduce(rank[:, :], beats[:, :, :], AX.X, ALU.add))
                then(v_.scalar_tensor_tensor(gate[:, :], rank[:, :], 1.5, lexp[:, :], ALU.is_lt, ALU.mult))
                then(v_.tensor_scalar(gate_n[:, :], gate[:, :], lrec[:, 0:1], 0.5, ALU.mult, ALU.mult), 2 * KV - 5)
                v_.tensor_tensor(act_g[:, :, :], silu2[:, :, :],
                                 gate_n[:, :].unsqueeze(2).to_broadcast([P, NE, NI]), ALU.mult).then_inc(s_gate, KV)

            run_slots(dve, slot)

        @block.tensor
        def _(pe):
            t_ = nc.tensor

            def three(out, l_hi, l_lo, r_hi, r_lo, first, last):
                t_.matmul(out, l_hi, r_lo, start=first, stop=False)
                t_.matmul(out, l_lo, r_hi, start=False, stop=False)
                return t_.matmul(out, l_hi, r_hi, start=False, stop=last)

            def flip(out, src):
                return t_.matmul(out, src, ident[:, :], is_transpose=True, start=True, stop=True)

            def project(ps, l_hi, l_lo, c):
                for t in range(DT):
                    cols = slice(t * GRP, (t + 1) * GRP)
                    ins = three(ps[:, :], l_hi[:, t, :], l_lo[:, t, :], w_hi[:, c, cols], w_lo[:, c, cols],
                                t == 0, t == DT - 1)
                return ins

            def x_flip(g):
                pe.wait_ge(s_xn, g + KV)
                for t in range(DT):
                    ins = flip(ps_tr[:, t * P:(t + 1) * P], xn[:, t * P:(t + 1) * P])
                ins.then_inc(s_xTps, KV)

            def queries(g, p, s):
                after(pe, s_qsq, g)
                project(ps_q, xT_hi[p], xT_lo[p], wQ + s).then_inc(s_qps, 1)

            def kv_unit(g, p, u):
                if u == 0:
                    pe.wait_ge(s_chi, g + KV)
                    pe.wait_ge(s_clo, g + KV)
                if u == 1:
                    pe.wait_ge(s_xTlo, g + KV)
                l_hi, l_lo = (cT_hi, cT_lo) if u % 2 == 0 else (xT_hi[p], xT_lo[p])
                project(ps_kv, l_hi, l_lo, wK if u < 2 else wV).then_inc(s_kvps, 1)

            def k_flip(u):
                pe.wait_ge(s_kn, u)
                for h in range(KV):
                    ins = flip(ps_tr[:, h * P:(h + 1) * P], krot_n[:, h, :])
                ins.then_inc(s_kTps, 2)

            def q_flip(g):
                pe.wait_ge(s_qrot, g + 1)
                for h in range(REP):
                    ins = flip(ps_tr[:, h * P:(h + 1) * P], qrot[:, h, :])
                ins.then_inc(s_qTps, 1)

            def scores(g, p, s):
                pe.wait_ge(s_qTlo, g + 1)
                for h in range(REP):
                    if h % 2 == 0:
                        after(pe, s_exp[h // 2], g)
                    ins = three(ps_s[h // 2][:, (h % 2) * KEYS:(h % 2 + 1) * KEYS], qT_hi[:, h, :], qT_lo[:, h, :],
                                kT_hi[p][:, s, :], kT_lo[p][:, s, :], True, True)
                    if h % 2:
                        ins.then_inc(s_score[h // 2], 1)

            def p_flip(g):
                pe.wait_ge(s_pn_pool, g + 1)
                pe.wait_ge(s_pn_dve, g + 1)
                for t in range(2):
                    for h in range(REP):
                        ins = flip(ps_pT[t][:, h * P:(h + 1) * P], probs[:, h, t * P:(t + 1) * P])
                    ins.then_inc(s_pTps[t], 1)

            def values(g, p, s):
                cols = slice(s * HD, (s + 1) * HD)
                pe.wait_ge(s_pTlo[1], g + 1)
                pe.wait_ge(s_pTlo[0], g + 1)
                for t in range(2):
                    ins = three(ps_att[:, :], v_hi[p][:, t, cols], v_lo[p][:, t, cols], pT_hi[:, t, :],
                                pT_lo[:, t, :], t == 0, t == 1)
                ins.then_inc(s_att, 1)

            def output(g, s):
                pe.wait_ge(s_alo, g + 1)
                for h in range(REP):
                    cols = slice(h * D, (h + 1) * D)
                    ins = three(ps_o[:, 0:D], aT_hi[:, h, :], aT_lo[:, h, :], w_hi[:, wO + s, cols],
                                w_lo[:, wO + s, cols], s == 0 and h == 0, s == KV - 1 and h == REP - 1)
                ins.then_inc(s_wo, 1)

            pe.wait_ge(s_const, 4)
            x_flip(0)
            pe.wait_ge(s_wlo_pool, 1)
            kv_unit(0, 0, 0)
            pe.wait_ge(s_wlo_dve, 1)
            pe.wait_ge(s_xTlo, KV)
            queries(0, 0, 0)
            pe.wait_ge(s_ksq, 2)
            kv_unit(0, 0, 1)
            pe.wait_ge(s_wlo_pool, 2)
            pe.wait_ge(s_ksq, 4)
            kv_unit(0, 0, 2)
            k_flip(2)
            pe.wait_ge(s_vlo, 2)
            kv_unit(0, 0, 3)
            pe.wait_ge(s_kTlo, 2)
            k_flip(4)
            pe.wait_ge(s_kTlo, 4)
            q_flip(0)

            def slot(g, n):
                s, b, p = flags(n)
                nxt = b + 1 < B
                if n < GROUPS:
                    if s == 0:
                        pe.wait_ge(s_kTlo, g + KV)
                    scores(g, p, s)
                if n + 1 < GROUPS:
                    if n < 3:
                        pe.wait_ge(s_wlo_dve, (2, 3, 5)[n])
                    queries(g + 1, p if s < 3 else 1 - p, (s + 1) % KV)
                if 1 <= n <= GROUPS:
                    if s == 1:
                        pe.wait_ge(s_vlo, g - s + KV)
                    values(g - 1, p if s > 0 else 1 - p, (s - 1) % KV)
                if s in (1, 2) and nxt:
                    if s == 1:
                        pe.wait_ge(s_xTlo, g - s + 2 * KV)
                    elif b > 0:
                        pe.wait_ge(s_x2T, g - s)
                    k_flip(g - s + KV + 2 * s)
                if nxt:
                    if s == 0:
                        pe.wait_ge(s_vlo, g + KV)
                    if s == 1:
                        pe.wait_ge(s_ksq, g - s + KV + 2)
                        if b > 1:
                            pe.wait_ge(s_out, g - s - KV)
                    if s == 2:
                        pe.wait_ge(s_ksq, g - s + 2 * KV)
                    if s == 3:
                        pe.wait_ge(s_vlo, g - s + KV + 2)
                        after(pe, s_gate, g - s)
                    kv_unit(g - s + KV, 1 - p, s)
                if n + 1 < GROUPS:
                    if s in (1, 2) and nxt:
                        pe.wait_ge(s_kTlo, g - s + KV + 2 * s)
                    elif s == 0 and b > 1:
                        pe.wait_ge(s_agT, g - KV)
                    elif s == 2:
                        pe.wait_ge(s_x2T, g - s)
                    q_flip(g + 1)
                if 1 <= n <= GROUPS:
                    if s == 1 and b > 0:
                        pe.wait_ge(s_x2, g - s)
                    if n <= KV:
                        pe.wait_ge(s_wlo_dve, (4, 6, 7, 8)[n - 1])
                    output(g - 1, (s - 1) % KV)
                if s == 0 and nxt:
                    pe.wait_ge(s_qTlo, g + 2)
                    x_flip(g + KV)
                if s == 0 and 2 <= b <= B + 1:
                    if nxt:
                        pe.wait_ge(s_ksq, g + KV + 2)
                    elif b < B:
                        pe.wait_ge(s_vlo, g + KV)
                    pe.wait_ge(s_agT, g - KV)
                    t_.matmul(ps_kv[:, 0:D], agT[:, :], up_w[:, :], start=True, stop=True).then_inc(s_y, KV)
                if s == 1 and 1 <= b <= B:
                    if n + 1 < GROUPS:
                        pe.wait_ge(s_qTlo, g + 2)
                    else:
                        pe.wait_ge(s_agT, g - s - KV)
                    pe.wait_ge(s_xn2, g - s)
                    for t in range(DT):
                        ins = flip(ps_tr[:, t * P:(t + 1) * P], xn2[:, t * P:(t + 1) * P])
                    ins.then_inc(s_x2Tps, KV)
                if s == 2 and 1 <= b <= B:
                    if nxt:
                        pe.wait_ge(s_vlo, g - s + KV + 2)
                    else:
                        pe.wait_ge(s_out, g - s - KV)
                    if b == 1:
                        pe.wait_ge(s_small, 32)
                    pe.wait_ge(s_x2T, g - s)
                    for t in range(DT):
                        ins = t_.matmul(ps_kv[:, 0:NE + EI], x2T[:, t, :], ffn_in_w[:, t, :],
                                        start=t == 0, stop=t == DT - 1)
                    ins.then_inc(s_h, KV)
                if s == 3 and 1 <= b <= B:
                    if n + 1 < GROUPS:
                        pe.wait_ge(s_qTlo, g + 2)
                    pe.wait_ge(s_gate, g - s)
                    flip(ps_tr[:, 0:P], act_g[:, :, :].rearrange("p e i -> p (e i)")).then_inc(s_agTps, KV)
                if n < GROUPS:
                    after(pe, s_pTlo[0], g)
                    after(pe, s_pTlo[1], g)
                    p_flip(g)

            run_slots(pe, slot)


def kernel(**inputs):
    import concourse.bacc as bacc
    import numpy as np
    from concourse.bass_utils import run_bass_kernel_spmd

    def arr(name):
        return np.asarray(inputs[name])

    def heads_in(w):
        return w.reshape(-1, GRP, DT, P).transpose(0, 3, 2, 1).reshape(-1, P, CH)

    wo = arr("L0_xattn_Wo").reshape(D, KV, REP, HD).transpose(1, 3, 2, 0).reshape(KV, P, CH)
    weights = np.concatenate([heads_in(arr("L0_xattn_Wk")), heads_in(arr("L0_xattn_Wv")),
                              heads_in(arr("L0_xattn_Wq")), wo])
    positions = np.stack([arr("pos_BxS2"), arr("itok_BxS_4096_4607")], axis=1).reshape(2 * B, S).T
    experts_in = np.concatenate([arr("L0_ffn_router_w"), arr("L0_ffn_down_w").reshape(EI, D)])
    freq = (np.float32(1.0) / np.float32(10000.0) ** (np.arange(0, HD, 2, dtype=np.float32) / np.float32(HD)))
    data = {
        "x": arr("x"),
        "ctxT": arr("ctx_2048").reshape(B, S, DT, P).transpose(0, 3, 2, 1).reshape(B, P, DT * S),
        "positions": positions,
        "weights": weights,
        "norms": np.concatenate([arr("L0_xattn_q_norm_w"), arr("L0_xattn_k_norm_w")]),
        "experts_in": experts_in.reshape(NE + EI, DT, P).transpose(2, 1, 0),
        "experts_out": arr("L0_ffn_up_w").transpose(0, 2, 1).reshape(EI, D),
        "frequencies": freq.astype(np.float32),
    }
    data = {name: np.ascontiguousarray(a) for name, a in data.items()}
    nc = bacc.Bacc("TRN2", target_bir_lowering=False, num_devices=1)
    args = [nc.dram_tensor(f"in_{name}", a.shape, mybir.dt.from_np(a.dtype), kind="ExternalInput").ap()
            for name, a in data.items()]
    args.append(nc.dram_tensor("out", (B, S, D), F32, kind="ExternalOutput").ap())
    xattn_ffn(nc, *args)
    result = run_bass_kernel_spmd(nc, [{f"in_{name}": a for name, a in data.items()}], core_ids=[0])
    return result.results[0]["out"]
```

```python
import math
from contextlib import ExitStack

import concourse.bass as bass
from concourse import mybir

F32 = mybir.dt.float32
F32R = mybir.dt.float32r
I32 = mybir.dt.int32
ALU = mybir.AluOpType
ACT = mybir.ActivationFunctionType
AX = mybir.AxisListType

B, S, D = 8, 128, 256
HEADS, KV, HD = 16, 4, 128
REP = HEADS // KV
P = 128
DT = D // P
HALF = HD // 2
NE, NI = 8, 16
EI = NE * NI
GRP = REP * HD
KEYS = 2 * S
CH = DT * GRP
GROUPS = B * KV
RMS_EPS, LN_EPS = 1e-6, 1e-5

PAIR = 2 * KV
LOOP_FROM = PAIR + 1
LOOP_TO = GROUPS - PAIR + 1
TAIL_TO = GROUPS + KV + 1

MAGIC = 1.5 * 2.0 ** 23
TWO_PI = (6.28125, 0.0019350051879882812, 3.019916050561733e-07)
PI_F32 = 3.1415925


def after(engine, sem, count):
    if not (isinstance(count, int) and count <= 0):
        engine.wait_ge(sem, count)


def xattn_ffn(nc, x_d, ctxT_d, pos_d, w_d, norm_d, ffn_in_d, up_d, freq_d, out_d):
    x_rows = x_d.rearrange("b s d -> (b s) d")
    ctx_rows = ctxT_d.rearrange("b p n -> (b p) n")
    out_rows = out_d.rearrange("b s d -> (b s) d")

    with ExitStack() as ctx:
        def sb(name, shape, dt=F32):
            return ctx.enter_context(nc.sbuf_tensor(name, shape, dt))

        def sem(name):
            return ctx.enter_context(nc.semaphore(name))

        ident = sb("ident", [P, P])
        neg_half = sb("neg_half", [P, 8])
        earlier = sb("earlier", [P, NE, NE])
        ln_eps = sb("ln_eps", [P, 1])
        rms_eps = sb("rms_eps", [P, REP])
        half_pi = sb("half_pi", [P, 1])
        wK, wV, wQ, wO = 0, 1, 2, 6
        w_order = [wK, wQ, wV, wQ + 1, wQ + 2, wO, wQ + 3, wO + 1, wO + 2, wO + 3]
        RAW = 5
        w_raw = sb("w_raw", [P, RAW, CH])
        w_hi = sb("w_hi", [P, 10, CH], F32R)
        w_lo = sb("w_lo", [P, 10, CH], F32R)
        ffn_in_w = sb("ffn_in_w", [P, DT, NE + EI])
        up_w = sb("up_w", [P, D])
        norm_w = sb("norm_w", [P, 2, 2, HALF])
        norm_sw = sb("norm_sw", [P, 2, 2, HALF])
        freq = sb("freq", [P, HALF])
        pos_i = sb("pos_i", [P, 2 * B], I32)
        pos_f = sb("pos_f", [P, 2 * B])
        cos_t = sb("cos_t", [P, 2 * B * HALF])
        sin_t = sb("sin_t", [P, 2 * B * HALF])
        q_tab = [sb(f"q_tab{i}", [P, 2, 2, HALF]) for i in range(2)]
        k_tab = [sb(f"k_tab{i}", [P, 2, 2, 2, HALF]) for i in range(2)]
        x_ln = sb("x_ln", [P, D])
        x_res = sb("x_res", [P, D])
        x2 = sb("x2", [P, D])
        x_out = sb("x_out", [P, D])
        bn6 = sb("bn6", [P, 2, 6])
        mv = sb("mv", [P, 2, 2])
        ve = sb("ve", [P, 2])
        rstd = sb("rstd", [P, 2])
        xn = sb("xn", [P, D])
        xn2 = sb("xn2", [P, D])
        xT_hi = [sb(f"xT_hi{i}", [P, DT, P], F32R) for i in range(2)]
        xT_lo = [sb(f"xT_lo{i}", [P, DT, P], F32R) for i in range(2)]
        ctx_raw = sb("ctx_raw", [P, DT, P])
        cT_hi = sb("cT_hi", [P, DT, P], F32R)
        cT_lo = sb("cT_lo", [P, DT, P], F32R)
        kcos = sb("kcos", [P, KV, HD])
        ksin = sb("ksin", [P, KV, HD])
        krot = sb("krot", [P, KV, HD])
        krot_n = sb("krot_n", [P, KV, HD])
        kss = sb("kss", [P, KV])
        kve = sb("kve", [P, KV])
        krs = sb("krs", [P, KV])
        kT_hi = [sb(f"kT_hi{i}", [P, KV, KEYS], F32R) for i in range(2)]
        kT_lo = [sb(f"kT_lo{i}", [P, KV, KEYS], F32R) for i in range(2)]
        v_hi = [sb(f"v_hi{i}", [P, 2, KV * HD], F32R) for i in range(2)]
        v_lo = [sb(f"v_lo{i}", [P, 2, KV * HD], F32R) for i in range(2)]
        qprod = sb("qprod", [P, 2, REP, HD])
        qcos, qsin = qprod[:, 0], qprod[:, 1]
        qrot = sb("qrot", [P, REP, HD])
        qss = sb("qss", [P, REP])
        qve = sb("qve", [P, REP])
        qscale = sb("qscale", [P, REP])
        qT_hi = sb("qT_hi", [P, REP, P], F32R)
        qT_lo = sb("qT_lo", [P, REP, P], F32R)
        smax = sb("smax", [P, REP])
        sbias = sb("sbias", [P, REP])
        probs = sb("probs", [P, REP, KEYS])
        turns = qprod[:, :, :, :].rearrange("p k h d -> p (k h d)")
        ang = probs[:, :, :].rearrange("p h n -> p (h n)")
        psums = sb("psums", [P, REP])
        rsums = sb("rsums", [P, REP])
        pT_hi = sb("pT_hi", [P, 2, REP * P], F32R)
        pT_lo = sb("pT_lo", [P, 2, REP * P], F32R)
        aT_hi = sb("aT_hi", [P, REP, P], F32R)
        aT_lo = sb("aT_lo", [P, REP, P], F32R)
        x2T = sb("x2T", [P, DT, P])
        lmax = sb("lmax", [P, 1])
        lexp = sb("lexp", [P, NE])
        lsum = sb("lsum", [P, 1])
        lrec = sb("lrec", [P, 1])
        htanh = sb("htanh", [P, NE, NI])
        beats = sb("beats", [P, NE, NE])
        ties = sb("ties", [P, NE, NE])
        rank = sb("rank", [P, NE])
        gate = sb("gate", [P, NE])
        gate_n = sb("gate_n", [P, NE])
        silu2 = sb("silu2", [P, NE, NI])
        act_g = sb("act_g", [P, NE, NI])
        agT = sb("agT", [P, P])

        def bank(name):
            return ctx.enter_context(nc.psum_tensor(name, [P, 512], F32))
        ps_q = bank("ps_q")
        ps_kv = bank("ps_kv")
        ps_tr = bank("ps_tr")
        ps_s = [bank("ps_s0"), bank("ps_s1")]
        ps_pT = [bank("ps_pT0"), bank("ps_pT1")]
        ps_att = ps_pT[1]
        ps_o = bank("ps_o")

        s_pos, s_small, s_xln, s_ctx, s_xres, s_store = (
            sem(n) for n in ("pos_loaded", "small_loaded", "xln_loaded", "ctx_loaded", "xres_loaded", "out_stored"))
        s_w = [sem(f"w_loaded{i}") for i in range(10)]
        s_norm = sem("norm_weights_loaded")
        s_const = sem("constants_made")
        s_whi, s_wlo_dve, s_wlo_pool = sem("w_hi_made"), sem("w_lo_dve"), sem("w_lo_pool")
        s_posf, s_ang, s_abs, s_trig = sem("pos_float"), sem("angles_made"), sem("abs_made"), sem("trig_made")
        s_dve = sem("dve_chain")
        s_pool = sem("pool_chain")
        s_qtab, s_ktab = sem("q_tables_made"), sem("k_tables_made")
        s_bn, s_mv, s_rstd, s_xn = sem("ln_stats"), sem("ln_mean_var"), sem("ln_rstd"), sem("ln_done")
        s_ve = sem("ln_var_eps")
        s_bn2, s_mv2, s_rstd2, s_xn2 = sem("ln2_stats"), sem("ln2_mean_var"), sem("ln2_rstd"), sem("ln2_done")
        s_ve2 = sem("ln2_var_eps")
        s_xTps, s_xThi, s_xTlo = sem("xT_in_psum"), sem("xT_hi_made"), sem("xT_lo_made")
        s_chi, s_clo = sem("ctx_hi_made"), sem("ctx_lo_made")
        s_kvps, s_kprod, s_ksq = sem("kv_in_psum"), sem("k_products"), sem("k_squares")
        s_kadd, s_kve, s_krs, s_kn = sem("k_rotated"), sem("k_var_eps"), sem("k_rstd"), sem("k_normed")
        s_kTps, s_kThi, s_kTlo = sem("kT_in_psum"), sem("kT_hi_made"), sem("kT_lo_made")
        s_vhi, s_vlo = sem("v_hi_made"), sem("v_lo_made")
        s_qps, s_qprod, s_qsq = sem("q_in_psum"), sem("q_products"), sem("q_squares")
        s_qrot, s_qve, s_qscale = sem("q_rotated"), sem("q_var_eps"), sem("q_scale_made")
        s_qTps, s_qThi, s_qTlo = sem("qT_in_psum"), sem("qT_hi_made"), sem("qT_lo_made")
        s_score = [sem("scores0"), sem("scores1")]
        s_max = [sem("score_max0"), sem("score_max1")]
        s_bias = [sem("score_bias0"), sem("score_bias1")]
        s_exp = [sem("exp0"), sem("exp1")]
        s_rec, s_pn_pool, s_pn_dve = [sem("sum_reciprocals0"), sem("sum_reciprocals1")], sem("probs_scaled_pool"), sem("probs_scaled_dve")
        s_pTps = [sem("pT_in_psum0"), sem("pT_in_psum1")]
        s_pThi = [sem("pT_hi0"), sem("pT_hi1")]
        s_pTlo = [sem("pT_lo0"), sem("pT_lo1")]
        s_att, s_ahi, s_alo = sem("att_in_psum"), sem("att_hi_made"), sem("att_lo_made")
        s_wo = sem("projected")
        s_x2 = sem("residual_added")
        s_x2Tps, s_x2T = sem("x2T_in_psum"), sem("x2T_made")
        s_h, s_lmax, s_lact, s_silu, s_gate = sem("h_in_psum"), sem("logit_max"), sem("ffn_activated"), sem("ffn_silu"), sem("ffn_gated")
        s_f = sem("ffn_chain")
        s_agTps, s_agT = sem("agT_in_psum"), sem("agT_made")
        s_y, s_out = sem("y_in_psum"), sem("out_made")

        w_late = [(wQ + 2, wO), (wQ + 3, wO + 1), (wO + 2,), (wO + 3,)]
        w_dve = {0: (wQ + 2, 5), 1: (wQ + 3, 7)}
        w_pool = {0: (wO, 6), 1: (wO + 1, 8), 2: (wO + 2, 9), 3: (wO + 3, 10)}

        def raw(c):
            return w_raw[:, w_order.index(c) % RAW, :]

        def pair_cols(j):
            return slice(j * 2 * P, (j + 1) * 2 * P)

        def flags(n):
            s, b = n % KV, n // KV
            return s, b, b % 2

        def run_slots(engine, slot):
            for n in range(LOOP_FROM):
                slot(n, n)
            with engine.Fori(0, (LOOP_TO - LOOP_FROM) // PAIR) as turn:
                first = engine.snap(turn * PAIR + LOOP_FROM)
                for i in range(PAIR):
                    slot(first + i, LOOP_FROM + i)
            for n in range(LOOP_TO, TAIL_TO):
                slot(n, n)

        block = ctx.enter_context(nc.Block())

        @block.sync
        def _(sp):
            def load_ctx(r, first=False):
                sp.dma_start(ctx_raw[:, :, :], ctx_rows[r, :].rearrange("p (t n) -> p t n", t=DT)).then_inc(s_ctx, 16)

            def load_w(c):
                sp.dma_start(raw(c), w_d[c]).then_inc(s_w[c], 16)

            sp.dma_start(pos_i[:, :], pos_d).then_inc(s_pos, 16)
            sp.dma_start(freq[:, :], freq_d.partition_broadcast(P)).then_inc(s_pos, 16)
            sp.dma_start(x_ln[:, :], x_rows[0:P, :]).then_inc(s_xln, 16)
            load_ctx(slice(0, P))
            for c in w_order[:3]:
                load_w(c)
            sp.dma_start(norm_w[:, :, :, :].rearrange("p a h f -> p (a h f)"),
                         norm_d.partition_broadcast(P)).then_inc(s_norm, 16)
            for c in w_order[3:RAW]:
                load_w(c)
            sp.dma_start(ffn_in_w[:, :, :], ffn_in_d).then_inc(s_small, 16)
            sp.dma_start(up_w[:, :], up_d).then_inc(s_small, 16)
            sp.wait_ge(s_xn, KV)
            sp.dma_start(x_ln[:, :], x_rows[P:2 * P, :]).then_inc(s_xln, 16)
            sp.wait_ge(s_chi, KV)
            sp.wait_ge(s_clo, KV)
            load_ctx(slice(P, 2 * P))

            split_by = (s_wlo_pool, s_wlo_dve, s_wlo_pool, s_wlo_dve, s_wlo_dve)
            for c, split, count in zip(w_order[RAW:], split_by, (1, 1, 2, 2, 3)):
                sp.wait_ge(split, count)
                load_w(c)

            def step(g, b):
                row = g * (P // KV)

                def rows(ahead):
                    at = row + ahead * P
                    return slice(at, at + P) if isinstance(at, int) else bass.ds(at, P)
                if b + 2 < B:
                    sp.wait_ge(s_xn, g + 2 * KV)
                    sp.dma_start(x_ln[:, :], x_rows[rows(2), :]).then_inc(s_xln, 16)
                if b < B:
                    after(sp, s_x2, g)
                    sp.dma_start(x_res[:, :], x_rows[rows(0), :]).then_inc(s_xres, 16)
                if b + 2 < B:
                    sp.wait_ge(s_chi, g + 2 * KV)
                    sp.wait_ge(s_clo, g + 2 * KV)
                    load_ctx(rows(2))
                if b >= 2:
                    sp.wait_ge(s_out, g - KV)
                    sp.dma_start(out_rows[rows(-2), :], x_out[:, :]).then_inc(s_store, 16)

            for b in range(2):
                step(KV * b, b)
            with sp.Fori(0, B - 4) as turn:
                step(sp.snap(turn * KV + 2 * KV), 2)
            for b in range(B - 2, B + 2):
                step(KV * b, b)
            sp.wait_ge(s_store, 16 * B)

        @block.gpsimd
        def _(pool):
            g_ = nc.gpsimd
            count = [0]

            def link(ins):
                count[0] += 1
                ins.then_inc(s_pool, 1)
                pool.wait_ge(s_pool, count[0])

            g_.memset(neg_half[:, :], -0.5).then_inc(s_const, 1)
            g_.memset(ln_eps[:, :], LN_EPS)
            g_.memset(rms_eps[:, :], HD * RMS_EPS)
            g_.memset(half_pi[:, :], math.pi / 2).then_inc(s_const, 1)
            link(g_.memset(ident[:, :], 0.0))
            g_.affine_select(out=ident[:, :], in_=ident[:, :], compare_op=ALU.not_equal, fill=1.0, base=0,
                             pattern=[[-1, P]], channel_multiplier=1).then_inc(s_const, 1)
            link(g_.memset(earlier[:, :, :], 1.0))
            g_.affine_select(out=earlier[:, :, :], in_=earlier[:, :, :], compare_op=ALU.is_gt, fill=0.0, base=0,
                             pattern=[[1, NE], [-1, NE]], channel_multiplier=0).then_inc(s_const, 1)
            pool.wait_ge(s_const, 4)

            def ctx_lo(b16, b4):
                after(pool, s_ctx, b16)
                after(pool, s_chi, b4)
                g_.tensor_tensor(cT_lo[:, :, :], ctx_raw[:, :, :], cT_hi[:, :, :].bitcast(F32),
                                 ALU.subtract).then_inc(s_clo, KV)

            def w_lo_pool(c, n):
                pool.wait_ge(s_whi, n)
                g_.tensor_tensor(w_lo[:, c, :], raw(c), w_hi[:, c, :].bitcast(F32),
                                 ALU.subtract).then_inc(s_wlo_pool, 1)

            def tables(g, tile, dst, which, done, inc):
                at = g * (2 * HALF // KV) + tile * HALF
                cols = slice(at, at + HALF) if isinstance(at, int) else bass.ds(at, HALF)
                for kind, t, w in ((0, cos_t, norm_w), (1, sin_t, norm_sw)):
                    src = t[:, cols].unsqueeze(1).to_broadcast([P, 2, HALF])
                    g_.tensor_tensor(dst[:, kind, :, :], w[:, which, :, :], src, ALU.mult).then_inc(done, inc)

            def q_tables(g, p):
                tables(g, 1, q_tab[p], 0, s_qtab, KV // 2)

            def k_tables(g, p):
                for tile in range(2):
                    tables(g, tile, k_tab[p][:, tile], 1, s_ktab, KV // 4)

            def rsqrt(var, src, dst, done_add, done, eps, cols, n_add, step):
                g_.tensor_tensor(var, src, eps[:, 0:cols], ALU.add).then_inc(done_add, step)
                pool.wait_ge(done_add, n_add)
                g_.tensor_tensor(dst, var, neg_half[:, 0:cols], ALU.pow).then_inc(done, step)

            def ln1(g):
                pool.wait_ge(s_mv, g + KV)
                rsqrt(ve[:, 0:1], mv[:, 0, 1:2], rstd[:, 0:1], s_ve, s_rstd, ln_eps, 1, g + KV, KV)

            def rotate(out, c, s_):
                g_.tensor_tensor(out[:, :, 0:HALF], c[:, :, 0:HALF], s_[:, :, HALF:HD], ALU.add)
                return g_.tensor_tensor(out[:, :, HALF:HD], c[:, :, HALF:HD], s_[:, :, 0:HALF], ALU.add)

            def q_add(g):
                pool.wait_ge(s_qprod, g + 1)
                rotate(qrot, qcos, qsin).then_inc(s_qrot, 1)

            def q_scale(g):
                pool.wait_ge(s_qsq, g + 1)
                rsqrt(qve[:, :], qss[:, :], qscale[:, :], s_qve, s_qscale, rms_eps, REP, g + 1, 1)

            def k_unit(u):
                half = 2
                pool.wait_ge(s_kprod, u)
                rotate(krot, kcos, ksin).then_inc(s_kadd, half)
                pool.wait_ge(s_ksq, u)
                rsqrt(kve[:, :], kss[:, :], krs[:, :], s_kve, s_krs, rms_eps, KV, u, half)
                pool.wait_ge(s_kadd, u)
                pool.wait_ge(s_krs, u)
                g_.tensor_tensor(krot_n[:, :, :], krot[:, :, :],
                                 krs[:, :].unsqueeze(2).to_broadcast([P, KV, HD]), ALU.mult).then_inc(s_kn, half)

            def scale_probs(g):
                pool.wait_ge(s_rec[1], g + 1)
                g_.tensor_tensor(probs[:, 2:4, :], probs[:, 2:4, :],
                                 rsums[:, 2:4].unsqueeze(2).to_broadcast([P, 2, KEYS]), ALU.mult).then_inc(s_pn_pool, 1)

            ctx_lo(16, KV)
            w_lo_pool(wK, 1)
            ln1(0)
            w_lo_pool(wV, 3)
            pool.wait_ge(s_norm, 16)
            link(g_.tensor_scalar(norm_w[:, 1, :, :], norm_w[:, 1, :, :], math.sqrt(HD), 1.0, ALU.mult, ALU.mult))
            link(g_.tensor_scalar(norm_sw[:, :, 0, :], norm_w[:, :, 0, :], 1.0, 1.0, ALU.mult, ALU.mult))
            link(g_.tensor_scalar(norm_sw[:, :, 1, :], norm_w[:, :, 1, :], -1.0, 1.0, ALU.mult, ALU.mult))
            pool.wait_ge(s_trig, 2)
            k_tables(0, 0)
            q_tables(0, 0)
            k_unit(2)
            q_add(0)
            pool.wait_ge(s_kTps, 2)
            k_unit(4)
            q_scale(0)
            ln1(KV)
            pool.wait_ge(s_kvps, 3)
            ctx_lo(32, 2 * KV)
            k_tables(KV, 1)

            def slot(g, n):
                s, b, p = flags(n)
                if n + 1 < GROUPS:
                    q_add(g + 1)
                if n < GROUPS:
                    scale_probs(g)
                if s == 1 and 1 <= b <= B:
                    pool.wait_ge(s_mv2, g - s)
                    rsqrt(ve[:, 1:2], mv[:, 1, 1:2], rstd[:, 1:2], s_ve2, s_rstd2, ln_eps, 1, g - s, KV)
                if n + 1 < GROUPS:
                    q_scale(g + 1)
                if n in w_pool:
                    w_lo_pool(*w_pool[n])
                if s < 2 and b + 1 < B:
                    k_unit(g - s + KV + 2 * (s + 1))
                if s == 2 and b + 2 < B:
                    ln1(g - s + 2 * KV)
                if s == 2 and b + 1 < B:
                    q_tables(g - s + KV, 1 - p)
                if s == 2 and b + 2 < B:
                    k_tables(g - s + 2 * KV, p)
                if s == 3 and b + 2 < B:
                    pool.wait_ge(s_kvps, g - s + KV + 3)
                    ctx_lo((g - s + 3 * KV) * 4, g - s + 3 * KV)

            run_slots(pool, slot)

        @block.scalar
        def _(act):
            a_ = nc.scalar

            def copy(dst, src):
                return a_.activation(dst, src, ACT.Copy)

            def split_w(c):
                act.wait_ge(s_w[c], 16)
                copy(w_hi[:, c, :], raw(c)).then_inc(s_whi, 1)

            def ctx_hi(b16):
                act.wait_ge(s_ctx, b16)
                copy(cT_hi[:, :, :], ctx_raw[:, :, :]).then_inc(s_chi, KV)

            def x_hi(g, p):
                act.wait_ge(s_xTps, g + KV)
                copy(xT_hi[p][:, :, :].rearrange("p t n -> p (t n)"), ps_tr[:, 0:D]).then_inc(s_xThi, KV)

            def squares(ps, ss, done, inc):
                for h in range(REP):
                    head = ps[:, h * HD:(h + 1) * HD]
                    ins = a_.activation(head, head, ACT.Square,
                                        accum_out=ss[:, h:h + 1])
                ins.then_inc(done, inc)

            def q_squares(g):
                act.wait_ge(s_qprod, g + 1)
                squares(ps_q, qss, s_qsq, 1)

            def k_squares(u):
                act.wait_ge(s_kprod, u)
                squares(ps_kv, kss, s_ksq, 2)

            def v_high(g, p, tile):
                act.wait_ge(s_kvps, g + 3 + tile)
                copy(v_hi[p][:, tile, :], ps_kv[:, :]).then_inc(s_vhi, 2)

            def k_high(u, p, tile):
                act.wait_ge(s_kTps, u)
                copy(kT_hi[p][:, :, tile * S:(tile + 1) * S],
                     ps_tr[:, :].rearrange("p (h n) -> p h n", h=KV)).then_inc(s_kThi, 2)

            def q_high(g):
                act.wait_ge(s_qTps, g + 1)
                copy(qT_hi[:, :, :].rearrange("p h n -> p (h n)"), ps_tr[:, :]).then_inc(s_qThi, 1)

            def p_high(g, j):
                act.wait_ge(s_pTps[j], g + 1)
                copy(pT_hi[:, :, pair_cols(j)],
                     ps_pT[j][:, :].rearrange("p (t n) -> p t n", t=2)).then_inc(s_pThi[j], 1)

            ctx_hi(16)
            split_w(wK)
            act.wait_ge(s_ang, 1)
            a_.activation(sin_t[:, :], ang[:, :], ACT.Sin).then_inc(s_trig, 1)
            a_.activation(turns[:, :], ang[:, :], ACT.Abs).then_inc(s_abs, 1)
            act.wait_ge(s_abs, 1)
            act.wait_ge(s_const, 4)
            a_.activation(cos_t[:, :], turns[:, :], ACT.Sin, bias=half_pi[:, 0:1],
                          scale=-1.0).then_inc(s_trig, 1)
            x_hi(0, 0)
            split_w(wQ)
            split_w(wV)
            k_squares(2)
            q_squares(0)
            act.wait_ge(s_kve, 2)
            k_squares(4)
            v_high(0, 0, 0)
            k_high(2, 0, 0)
            v_high(0, 0, 1)
            k_high(4, 0, 1)
            q_high(0)
            split_w(wQ + 1)
            act.wait_ge(s_kvps, 3)
            ctx_hi(32)

            def slot(g, n):
                s, b, p = flags(n)
                if s == 3 and 1 <= b <= B:
                    act.wait_ge(s_lmax, g - s)
                    a_.activation(lexp[:, :], ps_kv[:, 0:NE], ACT.Exp, bias=lmax[:, 0:1], accum_out=lsum[:, 0:1])
                    a_.activation(htanh[:, :, :].rearrange("p e i -> p (e i)"), ps_kv[:, NE:NE + EI], ACT.Tanh,
                                  scale=0.5).then_inc(s_lact, KV)
                for h in range(REP):
                    if n < GROUPS:
                        if h % 2 == 0:
                            act.wait_ge(s_bias[h // 2], g + 1)
                        ins = a_.activation(probs[:, h, :], ps_s[h // 2][:, (h % 2) * KEYS:(h % 2 + 1) * KEYS],
                                            ACT.Exp, bias=sbias[:, h:h + 1], scale=qscale[:, h:h + 1],
                                            accum_out=psums[:, h:h + 1])
                        if h % 2:
                            ins.then_inc(s_exp[h // 2], 1)
                if s in (1, 2) and b + 1 < B:
                    k_high(g - s + KV + 2 * s, 1 - p, s - 1)
                if s == 0 and 2 <= b <= B + 1:
                    act.wait_ge(s_agTps, g - KV)
                    copy(agT[:, :], ps_tr[:, 0:P]).then_inc(s_agT, KV)
                if 1 <= n <= GROUPS:
                    act.wait_ge(s_att, g)
                    copy(aT_hi[:, :, :].rearrange("p h n -> p (h n)"), ps_att[:, :]).then_inc(s_ahi, 1)
                if s == 2 and b + 1 < B:
                    v_high(g - s + KV, 1 - p, 0)
                if n + 1 < GROUPS:
                    q_squares(g + 1)
                    q_high(g + 1)
                if n < GROUPS:
                    p_high(g, 0)
                if s < 2 and b + 1 < B:
                    k_squares(g - s + KV + 2 * (s + 1))
                if s == 3 and b + 1 < B:
                    v_high(g - s + KV, 1 - p, 1)
                if n < len(w_late):
                    for c in w_late[n]:
                        split_w(c)
                if n < GROUPS:
                    p_high(g, 1)
                if s == 0 and b + 1 < B:
                    x_hi(g + KV, 1 - p)
                if s == 1 and 1 <= b <= B:
                    act.wait_ge(s_x2Tps, g - s)
                    copy(x2T[:, :, :].rearrange("p t n -> p (t n)"), ps_tr[:, 0:D]).then_inc(s_x2T, KV)
                if s == 3 and b + 2 < B:
                    act.wait_ge(s_kvps, g - s + KV + 3)
                    ctx_hi((g - s + 3 * KV) * 4)

            run_slots(act, slot)

        @block.vector
        def _(dve):
            v_ = nc.vector
            count = [0]

            def link(ins):
                count[0] += 1
                ins.then_inc(s_dve, 1)
                dve.wait_ge(s_dve, count[0])

            def low(dst, src, hi):
                return v_.tensor_tensor(dst, src, hi.bitcast(F32), ALU.subtract)

            def split_w(c, n):
                dve.wait_ge(s_whi, n)
                low(w_lo[:, c, :], raw(c), w_hi[:, c, :]).then_inc(s_wlo_dve, 1)

            def ln1(g):
                dve.wait_ge(s_xln, (g + KV) * 4)
                v_.bn_stats(bn6[:, 0, :], x_ln[:, :]).then_inc(s_bn, KV)

            def ln1_moments(g):
                v_.bn_aggr(mv[:, 0, :], bn6[:, 0, :]).then_inc(s_mv, KV)

            def ln1_apply(g):
                dve.wait_ge(s_rstd, g + KV)
                v_.tensor_scalar(xn[:, :], x_ln[:, :], mv[:, 0, 0:1], rstd[:, 0:1],
                                 ALU.subtract, ALU.mult).then_inc(s_xn, KV)

            def x_low(g, p):
                dve.wait_ge(s_xThi, g + KV)
                low(xT_lo[p][:, :, :].rearrange("p t n -> p (t n)"), ps_tr[:, 0:D],
                    xT_hi[p][:, :, :].rearrange("p t n -> p (t n)")).then_inc(s_xTlo, KV)

            def products(ps, tab, c, s_):
                src = ps[:, :].rearrange("p (h d) -> p h d", h=REP)
                for kind, dst in ((0, c), (1, s_)):
                    t = tab[:, kind, :, :].rearrange("p a f -> p (a f)").unsqueeze(1).to_broadcast([P, REP, HD])
                    ins = v_.tensor_tensor(dst[:, :, :], src, t, ALU.mult)
                return ins

            def q_products(g, p):
                dve.wait_ge(s_qps, g + 1)
                products(ps_q, q_tab[p], qcos, qsin).then_inc(s_qprod, 1)

            def k_products(g, p, tile):
                dve.wait_ge(s_kvps, g + 1 + tile)
                products(ps_kv, k_tab[p][:, tile], kcos, ksin).then_inc(s_kprod, 2)

            def v_low(g, p, tile):
                dve.wait_ge(s_vhi, g + 2 * (tile + 1))
                low(v_lo[p][:, tile, :], ps_kv[:, :], v_hi[p][:, tile, :]).then_inc(s_vlo, 2)

            def k_low(u, p, tile):
                dve.wait_ge(s_kThi, u)
                low(kT_lo[p][:, :, tile * S:(tile + 1) * S], ps_tr[:, :].rearrange("p (h n) -> p h n", h=KV),
                    kT_hi[p][:, :, tile * S:(tile + 1) * S]).then_inc(s_kTlo, 2)

            def q_low(g):
                dve.wait_ge(s_qThi, g + 1)
                low(qT_lo[:, :, :].rearrange("p h n -> p (h n)"), ps_tr[:, :],
                    qT_hi[:, :, :].rearrange("p h n -> p (h n)")).then_inc(s_qTlo, 1)

            dve.wait_ge(s_pos, 32)
            link(v_.tensor_copy(pos_f[:, :], pos_i[:, :]))
            link(v_.tensor_tensor(ang[:, :].rearrange("p (t f) -> p t f", f=HALF), pos_f[:, :].unsqueeze(2).to_broadcast([P, 2 * B, HALF]),
                                  freq[:, :].unsqueeze(1).to_broadcast([P, 2 * B, HALF]), ALU.mult))
            ln1(0)
            dve.wait_ge(s_bn, KV)
            ln1_moments(0)
            link(v_.tensor_scalar(turns[:, :], ang[:, :], 1.0 / (2 * math.pi), MAGIC, ALU.mult, ALU.add))
            link(v_.tensor_scalar(turns[:, :], turns[:, :], MAGIC, None, ALU.subtract))
            for part in TWO_PI:
                link(v_.scalar_tensor_tensor(ang[:, :], turns[:, :], -part, ang[:, :], ALU.mult, ALU.add))
            v_.tensor_scalar(ang[:, :], ang[:, :], PI_F32, -PI_F32, ALU.min, ALU.max).then_inc(s_ang, 1)
            ln1_apply(0)
            x_low(0, 0)
            split_w(wQ, 2)
            dve.wait_ge(s_ktab, KV)
            dve.wait_ge(s_qtab, KV)
            k_products(0, 0, 0)
            q_products(0, 0)
            dve.wait_ge(s_kadd, 2)
            k_products(0, 0, 1)
            v_low(0, 0, 0)
            k_low(2, 0, 0)
            ln1(KV)
            dve.wait_ge(s_bn, 2 * KV)
            ln1_moments(KV)
            v_low(0, 0, 1)
            k_low(4, 0, 1)
            q_low(0)
            split_w(wQ + 1, 4)
            ln1_apply(KV)

            def slot(g, n):
                s, b, p = flags(n)
                if s == 3 and 1 <= b <= B:
                    dve.wait_ge(s_h, g - s)
                    v_.tensor_reduce(lmax[:, 0:1], ps_kv[:, 0:NE], AX.X, ALU.max, negate=True).then_inc(s_lmax, KV)
                if n < GROUPS:
                    for t in range(2):
                        if s == 1 and t == 1 and b > 0:
                            dve.wait_ge(s_bn2, g - s)
                        dve.wait_ge(s_score[t], g + 1)
                        v_.tensor_reduce(smax[:, 2 * t:2 * t + 2],
                                         ps_s[t][:, :].rearrange("p (h n) -> p h n", h=2),
                                         AX.X, ALU.max, negate=True).then_inc(s_max[t], 1)
                if n < GROUPS:
                    dve.wait_ge(s_qscale, g + 1)
                    for t in range(2):
                        dve.wait_ge(s_max[t], g + 1)
                        pair = slice(2 * t, 2 * t + 2)
                        v_.tensor_tensor(sbias[:, pair], smax[:, pair], qscale[:, pair],
                                         ALU.mult).then_inc(s_bias[t], 1)
                if s == 1 and 1 <= b <= B:
                    if n > GROUPS:
                        dve.wait_ge(s_bn2, g - s)
                    v_.bn_aggr(mv[:, 1, :], bn6[:, 1, :]).then_inc(s_mv2, KV)
                gating = s == 3 and 1 <= b <= B
                if gating:
                    silu(g - s)
                    gate_step(g - s, 0)
                if s == 2 and b + 2 < B:
                    ln1(g - s + 2 * KV)
                if n + 1 < GROUPS:
                    if s == 3:
                        dve.wait_ge(s_qtab, g - s + 2 * KV)
                    if s == 2 and b + 2 < B:
                        dve.wait_ge(s_bn, g - s + 3 * KV)
                    q_products(g + 1, p if s < 3 else 1 - p)
                if s == 2 and b + 2 < B:
                    ln1_moments(g - s + 2 * KV)
                if gating:
                    gate_step(g - s, 1)
                if n < GROUPS:
                    reciprocals(g, 0)
                    dve.wait_ge(s_rec[0], g + 1)
                    for h in range(2):
                        ins = v_.tensor_scalar(probs[:, h, :], probs[:, h, :], rsums[:, h:h + 1], None, ALU.mult)
                    ins.then_inc(s_pn_dve, 1)
                if gating:
                    gate_step(g - s, 2)
                if n < GROUPS:
                    reciprocals(g, 1)
                if gating:
                    gate_step(g - s, 3)
                if s in (1, 2) and b + 1 < B:
                    k_low(g - s + KV + 2 * s, 1 - p, s - 1)
                if 1 <= n <= GROUPS:
                    dve.wait_ge(s_ahi, g)
                    low(aT_lo[:, :, :].rearrange("p h n -> p (h n)"), ps_att[:, :],
                        aT_hi[:, :, :].rearrange("p h n -> p (h n)")).then_inc(s_alo, 1)
                if gating:
                    gate_step(g - s, 4)
                if s < 2 and b + 1 < B:
                    if s == 0:
                        dve.wait_ge(s_ktab, g + 2 * KV)
                    k_products(g - s + KV, 1 - p, s)
                if s == 2 and b + 1 < B:
                    v_low(g - s + KV, 1 - p, 0)
                if gating:
                    gate_step(g - s, 5)
                if n + 1 < GROUPS:
                    q_low(g + 1)
                if gating:
                    gate_step(g - s, 6)
                if s == 1 and 1 <= b <= B:
                    dve.wait_ge(s_rstd2, g - s)
                    v_.tensor_scalar(xn2[:, :], x2[:, :], mv[:, 1, 0:1], rstd[:, 1:2],
                                     ALU.subtract, ALU.mult).then_inc(s_xn2, KV)
                if n < GROUPS:
                    p_low(g, 0)
                if s == 3 and b + 1 < B:
                    v_low(g - s + KV, 1 - p, 1)
                if s == 3 and b + 2 < B:
                    ln1_apply(g - s + 2 * KV)
                if s == 0 and 2 <= b <= B + 1:
                    dve.wait_ge(s_y, g - KV)
                    if b > 2:
                        dve.wait_ge(s_store, (g - 2 * KV) * 4)
                    v_.tensor_tensor(x_out[:, :], ps_q[:, 0:D], x2[:, :], ALU.add).then_inc(s_out, KV)
                if s == 0 and 1 <= b <= B:
                    dve.wait_ge(s_xres, g * 4)
                    dve.wait_ge(s_wo, g)
                    if b > 1:
                        dve.wait_ge(s_out, g - KV)
                    v_.tensor_tensor(x2[:, :], ps_o[:, 0:D], x_res[:, :], ALU.add).then_inc(s_x2, KV)
                    dve.wait_ge(s_x2, g)
                    v_.bn_stats(bn6[:, 1, :], x2[:, :]).then_inc(s_bn2, KV)
                if n in w_dve:
                    split_w(*w_dve[n])
                if n < GROUPS:
                    p_low(g, 1)
                if s == 0 and b + 1 < B:
                    x_low(g + KV, 1 - p)

            def p_low(g, j):
                dve.wait_ge(s_pThi[j], g + 1)
                low(pT_lo[:, :, pair_cols(j)], ps_pT[j][:, :].rearrange("p (t n) -> p t n", t=2),
                    pT_hi[:, :, pair_cols(j)]).then_inc(s_pTlo[j], 1)

            def reciprocals(g, pair):
                dve.wait_ge(s_exp[pair], g + 1)
                heads = slice(2 * pair, 2 * pair + 2)
                v_.reciprocal(rsums[:, heads], psums[:, heads]).then_inc(s_rec[pair], 1)

            def silu(g):
                dve.wait_ge(s_lact, g)
                v_.scalar_tensor_tensor(silu2[:, :, :].rearrange("p e i -> p (e i)"),
                                        htanh[:, :, :].rearrange("p e i -> p (e i)"), 1.0,
                                        ps_kv[:, NE:NE + EI], ALU.add, ALU.mult).then_inc(s_silu, KV)

            def gate_step(g, step):
                mine = lexp[:, :].unsqueeze(2).to_broadcast([P, NE, NE])
                other = lexp[:, :].unsqueeze(1).to_broadcast([P, NE, NE])
                if step > 0:
                    dve.wait_ge(s_f, (g - KV) * 2 + (2 * KV if step == 6 else step))
                if step == 0:
                    v_.tensor_tensor(beats[:, :, :], other, mine, ALU.is_gt)
                    v_.tensor_tensor(ties[:, :, :], other, mine, ALU.is_equal).then_inc(s_f, 1)
                if step == 1:
                    v_.tensor_tensor(ties[:, :, :], ties[:, :, :], earlier[:, :, :], ALU.mult)
                    v_.reciprocal(lrec[:, :], lsum[:, :]).then_inc(s_f, 1)
                if step == 2:
                    v_.tensor_tensor(beats[:, :, :], beats[:, :, :], ties[:, :, :], ALU.add).then_inc(s_f, 1)
                if step == 3:
                    v_.tensor_reduce(rank[:, :], beats[:, :, :], AX.X, ALU.add).then_inc(s_f, 1)
                if step == 4:
                    v_.scalar_tensor_tensor(gate[:, :], rank[:, :], 1.5, lexp[:, :],
                                            ALU.is_lt, ALU.mult).then_inc(s_f, 1)
                if step == 5:
                    v_.tensor_scalar(gate_n[:, :], gate[:, :], lrec[:, 0:1], 0.5,
                                     ALU.mult, ALU.mult).then_inc(s_f, 2 * KV - 5)
                if step == 6:
                    v_.tensor_tensor(act_g[:, :, :], silu2[:, :, :],
                                     gate_n[:, :].unsqueeze(2).to_broadcast([P, NE, NI]), ALU.mult).then_inc(s_gate, KV)

            run_slots(dve, slot)

        @block.tensor
        def _(pe):
            t_ = nc.tensor

            def three(out, l_hi, l_lo, r_hi, r_lo, first, last):
                t_.matmul(out, l_hi, r_lo, start=first, stop=False)
                t_.matmul(out, l_lo, r_hi, start=False, stop=False)
                return t_.matmul(out, l_hi, r_hi, start=False, stop=last)

            def flip(out, src):
                return t_.matmul(out, src, ident[:, :], is_transpose=True, start=True, stop=True)

            def project(ps, l_hi, l_lo, c):
                for t in range(DT):
                    cols = slice(t * GRP, (t + 1) * GRP)
                    ins = three(ps[:, :], l_hi[:, t, :], l_lo[:, t, :], w_hi[:, c, cols], w_lo[:, c, cols],
                                t == 0, t == DT - 1)
                return ins

            def x_flip(g):
                pe.wait_ge(s_xn, g + KV)
                for t in range(DT):
                    ins = flip(ps_tr[:, t * P:(t + 1) * P], xn[:, t * P:(t + 1) * P])
                ins.then_inc(s_xTps, KV)

            def queries(g, p, s):
                after(pe, s_qsq, g)
                project(ps_q, xT_hi[p], xT_lo[p], wQ + s).then_inc(s_qps, 1)

            def kv_unit(g, p, u):
                if u == 0:
                    pe.wait_ge(s_chi, g + KV)
                    pe.wait_ge(s_clo, g + KV)
                if u == 1:
                    pe.wait_ge(s_xTlo, g + KV)
                l_hi, l_lo = (cT_hi, cT_lo) if u % 2 == 0 else (xT_hi[p], xT_lo[p])
                project(ps_kv, l_hi, l_lo, wK if u < 2 else wV).then_inc(s_kvps, 1)

            def k_flip(u):
                pe.wait_ge(s_kn, u)
                for h in range(KV):
                    ins = flip(ps_tr[:, h * P:(h + 1) * P], krot_n[:, h, :])
                ins.then_inc(s_kTps, 2)

            def q_flip(g):
                pe.wait_ge(s_qrot, g + 1)
                for h in range(REP):
                    ins = flip(ps_tr[:, h * P:(h + 1) * P], qrot[:, h, :])
                ins.then_inc(s_qTps, 1)

            def scores(g, p, s):
                pe.wait_ge(s_qTlo, g + 1)
                for h in range(REP):
                    if h % 2 == 0:
                        after(pe, s_exp[h // 2], g)
                    ins = three(ps_s[h // 2][:, (h % 2) * KEYS:(h % 2 + 1) * KEYS], qT_hi[:, h, :], qT_lo[:, h, :],
                                kT_hi[p][:, s, :], kT_lo[p][:, s, :], True, True)
                    if h % 2:
                        ins.then_inc(s_score[h // 2], 1)

            def p_flip(g, j):
                for t in range(2):
                    for h in range(2):
                        at = (2 * t + h) * P
                        ins = flip(ps_pT[j][:, at:at + P], probs[:, 2 * j + h, t * P:(t + 1) * P])
                ins.then_inc(s_pTps[j], 1)

            def values(g, p, s):
                cols = slice(s * HD, (s + 1) * HD)
                pe.wait_ge(s_pTlo[1], g + 1)
                pe.wait_ge(s_pTlo[0], g + 1)
                for t in range(2):
                    ins = three(ps_att[:, :], v_hi[p][:, t, cols], v_lo[p][:, t, cols], pT_hi[:, t, :],
                                pT_lo[:, t, :], t == 0, t == 1)
                ins.then_inc(s_att, 1)

            def output(g, s):
                pe.wait_ge(s_alo, g + 1)
                for h in range(REP):
                    cols = slice(h * D, (h + 1) * D)
                    ins = three(ps_o[:, 0:D], aT_hi[:, h, :], aT_lo[:, h, :], w_hi[:, wO + s, cols],
                                w_lo[:, wO + s, cols], s == 0 and h == 0, s == KV - 1 and h == REP - 1)
                ins.then_inc(s_wo, 1)

            pe.wait_ge(s_const, 4)
            x_flip(0)
            pe.wait_ge(s_wlo_pool, 1)
            kv_unit(0, 0, 0)
            pe.wait_ge(s_wlo_dve, 1)
            pe.wait_ge(s_xTlo, KV)
            queries(0, 0, 0)
            pe.wait_ge(s_ksq, 2)
            kv_unit(0, 0, 1)
            pe.wait_ge(s_wlo_pool, 2)
            pe.wait_ge(s_ksq, 4)
            kv_unit(0, 0, 2)
            k_flip(2)
            pe.wait_ge(s_vlo, 2)
            kv_unit(0, 0, 3)
            pe.wait_ge(s_kTlo, 2)
            k_flip(4)
            pe.wait_ge(s_kTlo, 4)
            q_flip(0)

            def slot(g, n):
                s, b, p = flags(n)
                nxt = b + 1 < B
                if n < GROUPS:
                    if s == 0:
                        pe.wait_ge(s_kTlo, g + KV)
                    scores(g, p, s)
                if n + 1 < GROUPS:
                    if n < 3:
                        pe.wait_ge(s_wlo_dve, n + 2)
                    if s == 1 and b >= 2:
                        pe.wait_ge(s_out, g - s - KV)
                    queries(g + 1, p if s < 3 else 1 - p, (s + 1) % KV)
                if 1 <= n <= GROUPS:
                    if s == 1:
                        pe.wait_ge(s_vlo, g - s + KV)
                    values(g - 1, p if s > 0 else 1 - p, (s - 1) % KV)
                if s in (1, 2) and nxt:
                    if s == 1:
                        pe.wait_ge(s_xTlo, g - s + 2 * KV)
                    elif b > 0:
                        pe.wait_ge(s_x2T, g - s)
                    k_flip(g - s + KV + 2 * s)
                if s == 0 and 2 <= b <= B + 1:
                    pe.wait_ge(s_gate, g - KV)
                    flip(ps_tr[:, 0:P], act_g[:, :, :].rearrange("p e i -> p (e i)")).then_inc(s_agTps, KV)
                if nxt:
                    if s == 0:
                        pe.wait_ge(s_vlo, g + KV)
                    if s == 1:
                        pe.wait_ge(s_ksq, g - s + KV + 2)
                    if s == 2:
                        pe.wait_ge(s_ksq, g - s + 2 * KV)
                    if s == 3:
                        pe.wait_ge(s_vlo, g - s + KV + 2)
                        after(pe, s_silu, g - s)
                    kv_unit(g - s + KV, 1 - p, s)
                if n < GROUPS:
                    pe.wait_ge(s_pn_dve, g + 1)
                    p_flip(g, 0)
                if n + 1 < GROUPS:
                    if s in (1, 2) and nxt:
                        pe.wait_ge(s_kTlo, g - s + KV + 2 * s)
                    elif s == 0 and b > 1:
                        pe.wait_ge(s_agT, g - KV)
                    elif s == 2:
                        pe.wait_ge(s_x2T, g - s)
                    q_flip(g + 1)
                if 1 <= n <= GROUPS:
                    if s == 1 and b > 0:
                        pe.wait_ge(s_x2, g - s)
                    if n <= KV:
                        pe.wait_ge(s_wlo_pool, n + 2)
                    output(g - 1, (s - 1) % KV)
                if s == 0 and 2 <= b <= B + 1:
                    if n + 1 < GROUPS:
                        pe.wait_ge(s_qsq, g + 2)
                    pe.wait_ge(s_agT, g - KV)
                    t_.matmul(ps_q[:, 0:D], agT[:, :], up_w[:, :], start=True, stop=True).then_inc(s_y, KV)
                if n < GROUPS:
                    pe.wait_ge(s_pn_pool, g + 1)
                    p_flip(g, 1)
                if s == 0 and nxt:
                    pe.wait_ge(s_qTlo, g + 2)
                    x_flip(g + KV)
                if s == 1 and 1 <= b <= B:
                    if n + 1 < GROUPS:
                        pe.wait_ge(s_qTlo, g + 2)
                    else:
                        pe.wait_ge(s_agT, g - s - KV)
                    pe.wait_ge(s_xn2, g - s)
                    for t in range(DT):
                        ins = flip(ps_tr[:, t * P:(t + 1) * P], xn2[:, t * P:(t + 1) * P])
                    ins.then_inc(s_x2Tps, KV)
                if s == 2 and 1 <= b <= B:
                    if nxt:
                        pe.wait_ge(s_vlo, g - s + KV + 2)
                    else:
                        pe.wait_ge(s_silu, g - s - KV)
                    if b == 1:
                        pe.wait_ge(s_small, 32)
                    pe.wait_ge(s_x2T, g - s)
                    for t in range(DT):
                        ins = t_.matmul(ps_kv[:, 0:NE + EI], x2T[:, t, :], ffn_in_w[:, t, :],
                                        start=t == 0, stop=t == DT - 1)
                    ins.then_inc(s_h, KV)

            run_slots(pe, slot)


def kernel(**inputs):
    import concourse.bacc as bacc
    import numpy as np
    from concourse.bass_utils import run_bass_kernel_spmd

    def arr(name):
        return np.asarray(inputs[name])

    def heads_in(w):
        return w.reshape(-1, GRP, DT, P).transpose(0, 3, 2, 1).reshape(-1, P, CH)

    wo = arr("L0_xattn_Wo").reshape(D, KV, REP, HD).transpose(1, 3, 2, 0).reshape(KV, P, CH)
    weights = np.concatenate([heads_in(arr("L0_xattn_Wk")), heads_in(arr("L0_xattn_Wv")),
                              heads_in(arr("L0_xattn_Wq")), wo])
    positions = np.stack([arr("pos_BxS2"), arr("itok_BxS_4096_4607")], axis=1).reshape(2 * B, S).T
    experts_in = np.concatenate([arr("L0_ffn_router_w"), arr("L0_ffn_down_w").reshape(EI, D)])
    freq = (np.float32(1.0) / np.float32(10000.0) ** (np.arange(0, HD, 2, dtype=np.float32) / np.float32(HD)))
    data = {
        "x": arr("x"),
        "ctxT": arr("ctx_2048").reshape(B, S, DT, P).transpose(0, 3, 2, 1).reshape(B, P, DT * S),
        "positions": positions,
        "weights": weights,
        "norms": np.concatenate([arr("L0_xattn_q_norm_w"), arr("L0_xattn_k_norm_w")]),
        "experts_in": experts_in.reshape(NE + EI, DT, P).transpose(2, 1, 0),
        "experts_out": arr("L0_ffn_up_w").transpose(0, 2, 1).reshape(EI, D),
        "frequencies": freq.astype(np.float32),
    }
    data = {name: np.ascontiguousarray(a) for name, a in data.items()}
    nc = bacc.Bacc("TRN2", target_bir_lowering=False, num_devices=1)
    args = [nc.dram_tensor(f"in_{name}", a.shape, mybir.dt.from_np(a.dtype), kind="ExternalInput").ap()
            for name, a in data.items()]
    args.append(nc.dram_tensor("out", (B, S, D), F32, kind="ExternalOutput").ap())
    xattn_ffn(nc, *args)
    result = run_bass_kernel_spmd(nc, [{f"in_{name}": a for name, a in data.items()}], core_ids=[0])
    return result.results[0]["out"]
```

```python
import math
from contextlib import ExitStack

import concourse.bass as bass
from concourse import mybir

F32 = mybir.dt.float32
F32R = mybir.dt.float32r
I32 = mybir.dt.int32
ALU = mybir.AluOpType
ACT = mybir.ActivationFunctionType
AX = mybir.AxisListType

B, S, D = 8, 128, 256
HEADS, KV, HD = 16, 4, 128
REP = HEADS // KV
P = 128
DT = D // P
HALF = HD // 2
NE, NI = 8, 16
EI = NE * NI
GRP = REP * HD
KEYS = 2 * S
CH = DT * GRP
GROUPS = B * KV
RMS_EPS, LN_EPS = 1e-6, 1e-5

PAIR = 2 * KV
LOOP_FROM = PAIR + 1
LOOP_TO = GROUPS - PAIR + 1
TAIL_TO = GROUPS + KV + 1

MAGIC = 1.5 * 2.0 ** 23
TWO_PI = (6.28125, 0.0019350051879882812, 3.019916050561733e-07)
PI_F32 = 3.1415925


def after(engine, sem, count):
    if not (isinstance(count, int) and count <= 0):
        engine.wait_ge(sem, count)


def xattn_ffn(nc, x_d, ctxT_d, pos_d, w_d, norm_d, ffn_in_d, up_d, freq_d, out_d):
    x_rows = x_d.rearrange("b s d -> (b s) d")
    ctx_rows = ctxT_d.rearrange("b p n -> (b p) n")
    out_rows = out_d.rearrange("b s d -> (b s) d")

    with ExitStack() as ctx:
        def sb(name, shape, dt=F32):
            return ctx.enter_context(nc.sbuf_tensor(name, shape, dt))

        def sem(name):
            return ctx.enter_context(nc.semaphore(name))

        ident = sb("ident", [P, P])
        neg_half = sb("neg_half", [P, 8])
        earlier = sb("earlier", [P, NE, NE])
        ln_eps = sb("ln_eps", [P, 1])
        rms_eps = sb("rms_eps", [P, REP])
        half_pi = sb("half_pi", [P, 1])
        warm = sb("warm", [P, 2])
        wK, wV, wQ, wO = 0, 1, 2, 6
        w_order = [wK, wQ, wV, wQ + 1, wQ + 2, wO, wQ + 3, wO + 1, wO + 2, wO + 3]
        RAW = 5
        w_raw = sb("w_raw", [P, RAW, CH])
        w_hi = sb("w_hi", [P, 10, CH], F32R)
        w_lo = sb("w_lo", [P, 10, CH], F32R)
        ffn_in_w = sb("ffn_in_w", [P, DT, NE + EI])
        up_w = sb("up_w", [P, D])
        norm_w = sb("norm_w", [P, 2, 2, HALF])
        norm_sw = sb("norm_sw", [P, 2, 2, HALF])
        freq = sb("freq", [P, HALF])
        pos_i = sb("pos_i", [P, 2 * B], I32)
        pos_f = sb("pos_f", [P, 2 * B])
        cos_t = sb("cos_t", [P, 2 * B * HALF])
        sin_t = sb("sin_t", [P, 2 * B * HALF])
        q_tab = [sb(f"q_tab{i}", [P, 2, 2, HALF]) for i in range(2)]
        k_tab = [sb(f"k_tab{i}", [P, 2, 2, 2, HALF]) for i in range(2)]
        x_ln = sb("x_ln", [P, D])
        x_res = sb("x_res", [P, D])
        later_tokens = sb("later_tokens", [P, 3, D])
        x2, xn2, x_out = (later_tokens[:, i, :] for i in range(3))
        bn6 = sb("bn6", [P, 2, 6])
        mv = sb("mv", [P, 2, 2])
        ve = sb("ve", [P, 2])
        rstd = sb("rstd", [P, 2])
        xn = sb("xn", [P, D])
        xT_hi = [sb(f"xT_hi{i}", [P, DT, P], F32R) for i in range(2)]
        xT_lo = [sb(f"xT_lo{i}", [P, DT, P], F32R) for i in range(2)]
        ctx_raw = sb("ctx_raw", [P, DT, P])
        cT_hi = sb("cT_hi", [P, DT, P], F32R)
        cT_lo = sb("cT_lo", [P, DT, P], F32R)
        kcos = sb("kcos", [P, KV, HD])
        ksin = sb("ksin", [P, KV, HD])
        krot = sb("krot", [P, KV, HD])
        krot_n = sb("krot_n", [P, KV, HD])
        kss = sb("kss", [P, KV])
        kve = sb("kve", [P, KV])
        krs = sb("krs", [P, KV])
        kT_hi = [sb(f"kT_hi{i}", [P, KV, KEYS], F32R) for i in range(2)]
        kT_lo = [sb(f"kT_lo{i}", [P, KV, KEYS], F32R) for i in range(2)]
        v_hi = [sb(f"v_hi{i}", [P, 2, KV * HD], F32R) for i in range(2)]
        v_lo = [sb(f"v_lo{i}", [P, 2, KV * HD], F32R) for i in range(2)]
        qprod = sb("qprod", [P, 2, REP, HD])
        qcos, qsin = qprod[:, 0], qprod[:, 1]
        qrot = sb("qrot", [P, REP, HD])
        qss = sb("qss", [P, REP])
        qve = sb("qve", [P, REP])
        qscale = sb("qscale", [P, REP])
        qT_hi = sb("qT_hi", [P, REP, P], F32R)
        qT_lo = sb("qT_lo", [P, REP, P], F32R)
        smax = sb("smax", [P, REP])
        sbias = sb("sbias", [P, REP])
        probs = sb("probs", [P, REP, KEYS])
        ang = probs[:, :, :].rearrange("p h n -> p (h n)")
        psums = sb("psums", [P, REP])
        rsums = sb("rsums", [P, REP])
        pT_hi = sb("pT_hi", [P, 2, REP * P], F32R)
        pT_lo = sb("pT_lo", [P, 2, REP * P], F32R)
        aT_hi = sb("aT_hi", [P, REP, P], F32R)
        aT_lo = sb("aT_lo", [P, REP, P], F32R)
        x2T = sb("x2T", [P, DT, P])
        lmax = sb("lmax", [P, 1])
        lexp = sb("lexp", [P, NE])
        lsum = sb("lsum", [P, 1])
        lrec = sb("lrec", [P, 1])
        htanh = sb("htanh", [P, NE, NI])
        beats = sb("beats", [P, NE, NE])
        ties = sb("ties", [P, NE, NE])
        rank = sb("rank", [P, NE])
        gate = sb("gate", [P, NE])
        gate_n = sb("gate_n", [P, NE])
        silu2 = sb("silu2", [P, NE, NI])
        act_g = sb("act_g", [P, NE, NI])
        agT = sb("agT", [P, P])

        def bank(name):
            return ctx.enter_context(nc.psum_tensor(name, [P, 512], F32))
        ps_q = bank("ps_q")
        ps_kv = bank("ps_kv")
        ps_tr = bank("ps_tr")
        ps_s = [bank("ps_s0"), bank("ps_s1")]
        ps_pT = [bank("ps_pT0"), bank("ps_pT1")]
        ps_att = ps_pT[1]
        ps_o = bank("ps_o")

        s_pos, s_small, s_xln, s_ctx, s_xres, s_store = (
            sem(n) for n in ("pos_loaded", "small_loaded", "xln_loaded", "ctx_loaded", "xres_loaded", "out_stored"))
        s_w = [sem(f"w_loaded{i}") for i in range(10)]
        s_norm = sem("norm_weights_loaded")
        s_const = sem("constants_made")
        s_whi, s_wlo_dve, s_wlo_pool = sem("w_hi_made"), sem("w_lo_dve"), sem("w_lo_pool")
        s_posf, s_turns = sem("pos_float"), sem("later_turns_made")
        s_ang, s_abs, s_trig = sem("angles_made"), sem("abs_made"), sem("trig_made")
        s_dve = sem("dve_chain")
        s_pool = sem("pool_chain")
        s_qtab, s_ktab = sem("q_tables_made"), sem("k_tables_made")
        s_bn, s_mv, s_rstd, s_xn = sem("ln_stats"), sem("ln_mean_var"), sem("ln_rstd"), sem("ln_done")
        s_ve = sem("ln_var_eps")
        s_bn2, s_mv2, s_rstd2, s_xn2 = sem("ln2_stats"), sem("ln2_mean_var"), sem("ln2_rstd"), sem("ln2_done")
        s_ve2 = sem("ln2_var_eps")
        s_xTps, s_xThi, s_xTlo = sem("xT_in_psum"), sem("xT_hi_made"), sem("xT_lo_made")
        s_chi, s_clo = sem("ctx_hi_made"), sem("ctx_lo_made")
        s_kvps, s_kprod, s_ksq = sem("kv_in_psum"), sem("k_products"), sem("k_squares")
        s_kadd, s_kve, s_krs, s_kn = sem("k_rotated"), sem("k_var_eps"), sem("k_rstd"), sem("k_normed")
        s_kTps, s_kThi, s_kTlo = sem("kT_in_psum"), sem("kT_hi_made"), sem("kT_lo_made")
        s_vhi, s_vlo = sem("v_hi_made"), sem("v_lo_made")
        s_qps, s_qprod, s_qsq = sem("q_in_psum"), sem("q_products"), sem("q_squares")
        s_qrot, s_qve, s_qscale = sem("q_rotated"), sem("q_var_eps"), sem("q_scale_made")
        s_qTps, s_qThi, s_qTlo = sem("qT_in_psum"), sem("qT_hi_made"), sem("qT_lo_made")
        s_score = [sem("scores0"), sem("scores1")]
        s_max = [sem("score_max0"), sem("score_max1")]
        s_bias = [sem("score_bias0"), sem("score_bias1")]
        s_exp = [sem("exp0"), sem("exp1")]
        s_rec = [sem("sum_reciprocals0"), sem("sum_reciprocals1")]
        s_pn_pool, s_pn_dve = sem("probs_scaled_pool"), sem("probs_scaled_dve")
        s_pTps = [sem("pT_in_psum0"), sem("pT_in_psum1")]
        s_pThi = [sem("pT_hi0"), sem("pT_hi1")]
        s_pTlo = [sem("pT_lo0"), sem("pT_lo1")]
        s_att, s_ahi, s_alo = sem("att_in_psum"), sem("att_hi_made"), sem("att_lo_made")
        s_wo = sem("projected")
        s_x2 = sem("residual_added")
        s_x2Tps, s_x2T = sem("x2T_in_psum"), sem("x2T_made")
        s_h, s_lmax, s_lact = sem("h_in_psum"), sem("logit_max"), sem("ffn_activated")
        s_silu, s_gate, s_f = sem("ffn_silu"), sem("ffn_gated"), sem("ffn_gate_steps")
        s_agTps, s_agT = sem("agT_in_psum"), sem("agT_made")
        s_y, s_out = sem("y_in_psum"), sem("out_made")

        w_late = {0: (wQ + 3, wO + 1), 1: (wO + 2,), 2: (wO + 3,)}
        w_dve = {0: (wQ + 2, 5), 1: (wQ + 3, 7)}
        w_pool = {0: (wO + 1, 8), 1: (wO + 2, 9), 3: (wO + 3, 10)}

        first_trig, later_trig = slice(0, 4 * HALF), slice(4 * HALF, 2 * B * HALF)

        def turns(cols):
            if cols == first_trig:
                return x2T[:, :, :].rearrange("p t n -> p (t n)")
            return later_tokens[:, :, :].rearrange("p i d -> p (i d)")

        def angles(engine, link, cols):
            tiles = slice(cols.start // HALF, cols.stop // HALF)
            n = tiles.stop - tiles.start
            link(engine.tensor_tensor(ang[:, cols].rearrange("p (t f) -> p t f", f=HALF),
                                      pos_f[:, tiles].unsqueeze(2).to_broadcast([P, n, HALF]),
                                      freq[:, :].unsqueeze(1).to_broadcast([P, n, HALF]), ALU.mult))
            link(engine.tensor_scalar(turns(cols), ang[:, cols], 1.0 / (2 * math.pi), MAGIC, ALU.mult, ALU.add))

        def rotate(engine, out, c, s_):
            engine.tensor_tensor(out[:, :, 0:HALF], c[:, :, 0:HALF], s_[:, :, HALF:HD], ALU.add)
            return engine.tensor_tensor(out[:, :, HALF:HD], c[:, :, HALF:HD], s_[:, :, 0:HALF], ALU.add)

        def raw(c):
            return w_raw[:, w_order.index(c) % RAW, :]

        def early_att(n):
            return 1 <= n < GROUPS and n % KV < 2

        def pair_cols(j):
            return slice(j * 2 * P, (j + 1) * 2 * P)

        def flags(n):
            s, b = n % KV, n // KV
            return s, b, b % 2

        def run_slots(engine, slot):
            for n in range(LOOP_FROM):
                slot(n, n)
            with engine.Fori(0, (LOOP_TO - LOOP_FROM) // PAIR) as turn:
                first = engine.snap(turn * PAIR + LOOP_FROM)
                for i in range(PAIR):
                    slot(first + i, LOOP_FROM + i)
            for n in range(LOOP_TO, TAIL_TO):
                slot(n, n)

        block = ctx.enter_context(nc.Block())

        @block.sync
        def _(sp):
            def load_ctx(r):
                sp.dma_start(ctx_raw[:, :, :], ctx_rows[r, :].rearrange("p (t n) -> p t n", t=DT)).then_inc(s_ctx, 16)

            def load_w(c):
                sp.dma_start(raw(c), w_d[c]).then_inc(s_w[c], 16)

            sp.dma_start(pos_i[:, :], pos_d).then_inc(s_pos, 16)
            sp.dma_start(freq[:, :], freq_d.partition_broadcast(P)).then_inc(s_pos, 16)
            sp.dma_start(x_ln[:, :], x_rows[0:P, :]).then_inc(s_xln, 16)
            load_ctx(slice(0, P))
            load_w(w_order[0])
            sp.dma_start(norm_w[:, :, :, :].rearrange("p a h f -> p (a h f)"),
                         norm_d.partition_broadcast(P)).then_inc(s_norm, 16)
            for c in w_order[1:RAW]:
                load_w(c)
            sp.dma_start(ffn_in_w[:, :, :], ffn_in_d).then_inc(s_small, 16)
            sp.dma_start(up_w[:, :], up_d).then_inc(s_small, 16)
            sp.wait_ge(s_xn, KV)
            sp.dma_start(x_ln[:, :], x_rows[P:2 * P, :]).then_inc(s_xln, 16)
            sp.wait_ge(s_chi, KV)
            sp.wait_ge(s_clo, KV)
            load_ctx(slice(P, 2 * P))

            split_by = ((s_wlo_dve, 1), (s_wlo_pool, 1), (s_wlo_dve, 2), (s_wlo_pool, 2), (s_wlo_dve, 4))
            for c, (split, count) in zip(w_order[RAW:], split_by):
                sp.wait_ge(split, count)
                load_w(c)

            def step(g, b):
                row = g * (P // KV)

                def rows(ahead):
                    at = row + ahead * P
                    return slice(at, at + P) if isinstance(at, int) else bass.ds(at, P)
                if b + 2 < B:
                    sp.wait_ge(s_xn, g + 2 * KV)
                    sp.dma_start(x_ln[:, :], x_rows[rows(2), :]).then_inc(s_xln, 16)
                if b < B:
                    after(sp, s_x2, g)
                    sp.dma_start(x_res[:, :], x_rows[rows(0), :]).then_inc(s_xres, 16)
                if b + 2 < B:
                    sp.wait_ge(s_chi, g + 2 * KV)
                    sp.wait_ge(s_clo, g + 2 * KV)
                    load_ctx(rows(2))
                if b >= 2:
                    sp.wait_ge(s_out, g - KV)
                    sp.dma_start(out_rows[rows(-2), :], x_out[:, :]).then_inc(s_store, 16)

            for b in range(2):
                step(KV * b, b)
            with sp.Fori(0, B - 4) as turn:
                step(sp.snap(turn * KV + 2 * KV), 2)
            for b in range(B - 2, B + 2):
                step(KV * b, b)
            sp.wait_ge(s_store, 16 * B)

        @block.gpsimd
        def _(pool):
            g_ = nc.gpsimd
            count = [0]

            def link(ins):
                count[0] += 1
                ins.then_inc(s_pool, 1)
                pool.wait_ge(s_pool, count[0])

            g_.memset(neg_half[:, :], -0.5).then_inc(s_const, 1)
            g_.memset(ln_eps[:, :], LN_EPS)
            g_.memset(rms_eps[:, :], HD * RMS_EPS)
            g_.memset(half_pi[:, :], math.pi / 2).then_inc(s_const, 1)
            link(g_.memset(ident[:, :], 0.0))
            g_.affine_select(out=ident[:, :], in_=ident[:, :], compare_op=ALU.not_equal, fill=1.0, base=0,
                             pattern=[[-1, P]], channel_multiplier=1).then_inc(s_const, 1)
            link(g_.memset(earlier[:, :, :], 1.0))
            g_.affine_select(out=earlier[:, :, :], in_=earlier[:, :, :], compare_op=ALU.is_gt, fill=0.0, base=0,
                             pattern=[[1, NE], [-1, NE]], channel_multiplier=0).then_inc(s_const, 1)
            pool.wait_ge(s_const, 4)

            half = 2

            def ctx_lo(b16, b4):
                pool.wait_ge(s_ctx, b16)
                pool.wait_ge(s_chi, b4)
                g_.tensor_tensor(cT_lo[:, :, :], ctx_raw[:, :, :], cT_hi[:, :, :].bitcast(F32),
                                 ALU.subtract).then_inc(s_clo, KV)

            def w_lo_pool(c, n):
                pool.wait_ge(s_whi, n)
                g_.tensor_tensor(w_lo[:, c, :], raw(c), w_hi[:, c, :].bitcast(F32),
                                 ALU.subtract).then_inc(s_wlo_pool, 1)

            def tables(g, tile, dst, which, done, inc):
                at = g * (2 * HALF // KV) + tile * HALF
                cols = slice(at, at + HALF) if isinstance(at, int) else bass.ds(at, HALF)
                for kind, t, w in ((0, cos_t, norm_w), (1, sin_t, norm_sw)):
                    src = t[:, cols].unsqueeze(1).to_broadcast([P, 2, HALF])
                    g_.tensor_tensor(dst[:, kind, :, :], w[:, which, :, :], src, ALU.mult).then_inc(done, inc)

            def q_tables(g, p):
                tables(g, 1, q_tab[p], 0, s_qtab, KV // 2)

            def k_tables(g, p):
                for tile in range(2):
                    tables(g, tile, k_tab[p][:, tile], 1, s_ktab, KV // 4)

            def rsqrt(var, src, dst, done_add, done, eps, cols, n_add, step):
                g_.tensor_tensor(var, src, eps[:, 0:cols], ALU.add).then_inc(done_add, step)
                pool.wait_ge(done_add, n_add)
                g_.tensor_tensor(dst, var, neg_half[:, 0:cols], ALU.pow).then_inc(done, step)

            def ln1(g):
                pool.wait_ge(s_mv, g + KV)
                rsqrt(ve[:, 0:1], mv[:, 0, 1:2], rstd[:, 0:1], s_ve, s_rstd, ln_eps, 1, g + KV, KV)

            def q_add(g):
                pool.wait_ge(s_qprod, g + 1)
                rotate(g_, qrot, qcos, qsin).then_inc(s_qrot, 1)

            def q_scale(g):
                pool.wait_ge(s_qsq, g + 1)
                rsqrt(qve[:, :], qss[:, :], qscale[:, :], s_qve, s_qscale, rms_eps, REP, g + 1, 1)

            def k_rms(u):
                pool.wait_ge(s_ksq, u)
                rsqrt(kve[:, :], kss[:, :], krs[:, :], s_kve, s_krs, rms_eps, KV, u, half)

            def k_norm(u):
                pool.wait_ge(s_kadd, u)
                pool.wait_ge(s_krs, u)
                g_.tensor_tensor(krot_n[:, :, :], krot[:, :, :],
                                 krs[:, :].unsqueeze(2).to_broadcast([P, KV, HD]), ALU.mult).then_inc(s_kn, half)

            def k_rotate(u):
                pool.wait_ge(s_kprod, u)
                rotate(g_, krot, kcos, ksin).then_inc(s_kadd, half)

            def scale_probs(g):
                pool.wait_ge(s_rec[1], g + 1)
                g_.tensor_tensor(probs[:, 2:4, :], probs[:, 2:4, :],
                                 rsums[:, 2:4].unsqueeze(2).to_broadcast([P, 2, KEYS]), ALU.mult).then_inc(s_pn_pool, 1)

            pool.wait_ge(s_posf, 1)
            pool.wait_ge(s_pos, 32)
            angles(g_, link, later_trig)
            g_.tensor_scalar(turns(later_trig), turns(later_trig), 1.0, -MAGIC,
                             ALU.mult, ALU.add).then_inc(s_turns, 1)
            ln1(0)
            pool.wait_ge(s_norm, 16)
            link(g_.tensor_scalar(norm_w[:, 1, :, :], norm_w[:, 1, :, :], math.sqrt(HD), 1.0, ALU.mult, ALU.mult))
            link(g_.tensor_scalar(norm_sw[:, :, 0, :], norm_w[:, :, 0, :], 1.0, 1.0, ALU.mult, ALU.mult))
            link(g_.tensor_scalar(norm_sw[:, :, 1, :], norm_w[:, :, 1, :], -1.0, 1.0, ALU.mult, ALU.mult))
            pool.wait_ge(s_trig, 2)
            k_tables(0, 0)
            q_tables(0, 0)
            w_lo_pool(wQ, 2)
            k_rms(2)
            k_norm(2)
            k_rms(4)
            pool.wait_ge(s_kTps, 2)
            k_norm(4)
            q_scale(0)
            ln1(KV)
            w_lo_pool(wQ + 1, 4)
            pool.wait_ge(s_kvps, 3)
            ctx_lo(32, 2 * KV)
            k_tables(KV, 1)

            def slot(g, n):
                s, b, p = flags(n)
                if n + 1 < GROUPS:
                    q_add(g + 1)
                if n < GROUPS:
                    scale_probs(g)
                if s == 1 and 1 <= b <= B:
                    pool.wait_ge(s_mv2, g - s)
                    rsqrt(ve[:, 1:2], mv[:, 1, 1:2], rstd[:, 1:2], s_ve2, s_rstd2, ln_eps, 1, g - s, KV)
                if n + 1 < GROUPS:
                    q_scale(g + 1)
                if s < 2 and b + 1 < B:
                    k_rotate(g - s + KV + 2 * (s + 1))
                    k_rms(g - s + KV + 2 * (s + 1))
                if s == 0 and b + 1 < B:
                    k_norm(g + KV + 2)
                if s == 2 and b + 1 < B:
                    pool.wait_ge(s_kTps, g - s + KV + 2)
                    k_norm(g - s + KV + 4)
                if s == 2 and b + 2 < B:
                    ln1(g - s + 2 * KV)
                if s == 2 and b + 1 < B:
                    q_tables(g - s + KV, 1 - p)
                if n == 2:
                    pool.wait_ge(s_trig, 4)
                if s == 2 and b + 2 < B:
                    k_tables(g - s + 2 * KV, p)
                if s == 3 and b + 2 < B:
                    pool.wait_ge(s_kvps, g - s + KV + 3)
                    ctx_lo((g - s + 3 * KV) * 4, g - s + 3 * KV)
                if n in w_pool:
                    w_lo_pool(*w_pool[n])

            run_slots(pool, slot)

        @block.scalar
        def _(act):
            a_ = nc.scalar

            def copy(dst, src):
                return a_.activation(dst, src, ACT.Copy)

            def split_w(c):
                act.wait_ge(s_w[c], 16)
                copy(w_hi[:, c, :], raw(c)).then_inc(s_whi, 1)

            def ctx_hi(b16):
                act.wait_ge(s_ctx, b16)
                copy(cT_hi[:, :, :], ctx_raw[:, :, :]).then_inc(s_chi, KV)

            def x_hi(g, p):
                act.wait_ge(s_xTps, g + KV)
                copy(xT_hi[p][:, :, :].rearrange("p t n -> p (t n)"), ps_tr[:, 0:D]).then_inc(s_xThi, KV)

            def squares(ps, ss, done, inc):
                for h in range(REP):
                    head = ps[:, h * HD:(h + 1) * HD]
                    ins = a_.activation(head, head, ACT.Square,
                                        accum_out=ss[:, h:h + 1])
                ins.then_inc(done, inc)

            def q_squares(g):
                act.wait_ge(s_qprod, g + 1)
                squares(ps_q, qss, s_qsq, 1)

            def k_squares(u, ps=ps_kv):
                act.wait_ge(s_kprod, u)
                squares(ps, kss, s_ksq, 2)

            def v_high(g, p, tile, ps=ps_kv):
                act.wait_ge(s_kvps, g + 3 + tile)
                copy(v_hi[p][:, tile, :], ps[:, :]).then_inc(s_vhi, 2)

            def k_high(u, p, tile, ps=ps_tr):
                act.wait_ge(s_kTps, u)
                copy(kT_hi[p][:, :, tile * S:(tile + 1) * S],
                     ps[:, :].rearrange("p (h n) -> p h n", h=KV)).then_inc(s_kThi, 2)

            def q_high(g, ps=ps_tr):
                act.wait_ge(s_qTps, g + 1)
                copy(qT_hi[:, :, :].rearrange("p h n -> p (h n)"), ps[:, :]).then_inc(s_qThi, 1)

            def gated(g):
                act.wait_ge(s_agTps, g - KV)
                copy(agT[:, :], ps_tr[:, 0:P]).then_inc(s_agT, KV)

            def sines(cols, n):
                act.wait_ge(s_ang, n)
                a_.activation(sin_t[:, cols], ang[:, cols], ACT.Sin).then_inc(s_trig, 1)

            def cosines(cols, n):
                a_.activation(turns(cols), ang[:, cols], ACT.Abs).then_inc(s_abs, 1)
                act.wait_ge(s_abs, n)
                a_.activation(cos_t[:, cols], turns(cols), ACT.Sin, bias=half_pi[:, 0:1],
                              scale=-1.0).then_inc(s_trig, 1)

            def att_high(g):
                act.wait_ge(s_att, g)
                copy(aT_hi[:, :, :].rearrange("p h n -> p (h n)"), ps_att[:, :]).then_inc(s_ahi, 1)

            def p_high(g, j):
                act.wait_ge(s_pTps[j], g + 1)
                copy(pT_hi[:, :, pair_cols(j)],
                     ps_pT[j][:, :].rearrange("p (t n) -> p t n", t=2)).then_inc(s_pThi[j], 1)

            act.wait_ge(s_const, 4)
            a_.activation(warm[:, 0:1], half_pi[:, :], ACT.Sin)
            ctx_hi(16)
            split_w(wK)
            sines(first_trig, 1)
            cosines(first_trig, 1)
            x_hi(0, 0)
            split_w(wQ)
            split_w(wV)
            split_w(wQ + 1)
            k_squares(2)
            split_w(wQ + 2)
            act.wait_ge(s_kve, 2)
            k_squares(4, ps_s[0])
            split_w(wO)
            act.wait_ge(s_kvps, 3)
            ctx_hi(32)
            q_squares(0)
            k_high(2, 0, 0)
            v_high(0, 0, 0)
            v_high(0, 0, 1, ps_pT[0])
            q_high(0, ps_pT[1])
            k_high(4, 0, 1, ps_o)
            sines(later_trig, 2)
            cosines(later_trig, 2)
            a_.activation(warm[:, 1:2], half_pi[:, :], ACT.Exp)

            def slot(g, n):
                s, b, p = flags(n)
                if s == 3 and 1 <= b <= B:
                    act.wait_ge(s_lmax, g - s)
                    a_.activation(lexp[:, :], ps_kv[:, 0:NE], ACT.Exp, bias=lmax[:, 0:1], accum_out=lsum[:, 0:1])
                    a_.activation(htanh[:, :, :].rearrange("p e i -> p (e i)"), ps_kv[:, NE:NE + EI], ACT.Tanh,
                                  scale=0.5).then_inc(s_lact, KV)
                if s == 2 and 1 <= b <= B:
                    act.wait_ge(s_x2Tps, g - s)
                    copy(x2T[:, :, :].rearrange("p t n -> p (t n)"), ps_tr[:, 0:D]).then_inc(s_x2T, KV)
                for h in range(REP):
                    if n < GROUPS:
                        if h % 2 == 0:
                            act.wait_ge(s_bias[h // 2], g + 1)
                        ins = a_.activation(probs[:, h, :], ps_s[h // 2][:, (h % 2) * KEYS:(h % 2 + 1) * KEYS],
                                            ACT.Exp, bias=sbias[:, h:h + 1], scale=qscale[:, h:h + 1],
                                            accum_out=psums[:, h:h + 1])
                        if h % 2:
                            ins.then_inc(s_exp[h // 2], 1)
                    if h == 2 and early_att(n):
                        att_high(g)
                if s in (2, 3) and b + 1 < B:
                    k_high(g - s + KV + 2 * (s - 1), 1 - p, s - 2)
                if n == GROUPS:
                    gated(g)
                if 1 <= n <= GROUPS and not early_att(n):
                    att_high(g)
                if s == 0 and 2 <= b <= B + 1 and n != GROUPS:
                    gated(g)
                if s == 2 and b + 1 < B:
                    v_high(g - s + KV, 1 - p, 0)
                if n + 1 < GROUPS:
                    q_squares(g + 1)
                    q_high(g + 1)
                if n < GROUPS:
                    p_high(g, 0)
                if s < 2 and b + 1 < B:
                    k_squares(g - s + KV + 2 * (s + 1))
                if s == 3 and b + 1 < B:
                    v_high(g - s + KV, 1 - p, 1)
                if n < GROUPS:
                    p_high(g, 1)
                if s == 0 and b + 1 < B:
                    x_hi(g + KV, 1 - p)
                for c in w_late.get(n, ()):
                    split_w(c)
                if s == 3 and b + 2 < B:
                    act.wait_ge(s_kvps, g - s + KV + 3)
                    ctx_hi((g - s + 3 * KV) * 4)

            run_slots(act, slot)

        @block.vector
        def _(dve):
            v_ = nc.vector
            count = [0]

            def link(ins):
                count[0] += 1
                ins.then_inc(s_dve, 1)
                dve.wait_ge(s_dve, count[0])

            def low(dst, src, hi):
                return v_.tensor_tensor(dst, src, hi.bitcast(F32), ALU.subtract)

            def split_w(c, n):
                dve.wait_ge(s_whi, n)
                low(w_lo[:, c, :], raw(c), w_hi[:, c, :]).then_inc(s_wlo_dve, 1)

            def ln1(g):
                dve.wait_ge(s_xln, (g + KV) * 4)
                v_.bn_stats(bn6[:, 0, :], x_ln[:, :]).then_inc(s_bn, KV)

            def ln1_moments(g):
                v_.bn_aggr(mv[:, 0, :], bn6[:, 0, :]).then_inc(s_mv, KV)

            def ln1_apply(g):
                dve.wait_ge(s_rstd, g + KV)
                v_.tensor_scalar(xn[:, :], x_ln[:, :], mv[:, 0, 0:1], rstd[:, 0:1],
                                 ALU.subtract, ALU.mult).then_inc(s_xn, KV)

            def x_low(g, p):
                dve.wait_ge(s_xThi, g + KV)
                low(xT_lo[p][:, :, :].rearrange("p t n -> p (t n)"), ps_tr[:, 0:D],
                    xT_hi[p][:, :, :].rearrange("p t n -> p (t n)")).then_inc(s_xTlo, KV)

            def products(ps, tab, c, s_):
                src = ps[:, :].rearrange("p (h d) -> p h d", h=REP)
                for kind, dst in ((0, c), (1, s_)):
                    t = tab[:, kind, :, :].rearrange("p a f -> p (a f)").unsqueeze(1).to_broadcast([P, REP, HD])
                    ins = v_.tensor_tensor(dst[:, :, :], src, t, ALU.mult)
                return ins

            def q_products(g, p):
                dve.wait_ge(s_qps, g + 1)
                products(ps_q, q_tab[p], qcos, qsin).then_inc(s_qprod, 1)

            def k_products(g, p, tile, ps=ps_kv):
                dve.wait_ge(s_kvps, g + 1 + tile)
                products(ps, k_tab[p][:, tile], kcos, ksin).then_inc(s_kprod, 2)

            def v_low(g, p, tile, ps=ps_kv):
                dve.wait_ge(s_vhi, g + 2 * (tile + 1))
                low(v_lo[p][:, tile, :], ps[:, :], v_hi[p][:, tile, :]).then_inc(s_vlo, 2)

            def k_low(u, p, tile, ps=ps_tr):
                dve.wait_ge(s_kThi, u)
                low(kT_lo[p][:, :, tile * S:(tile + 1) * S], ps[:, :].rearrange("p (h n) -> p h n", h=KV),
                    kT_hi[p][:, :, tile * S:(tile + 1) * S]).then_inc(s_kTlo, 2)

            def q_low(g, ps=ps_tr):
                dve.wait_ge(s_qThi, g + 1)
                low(qT_lo[:, :, :].rearrange("p h n -> p (h n)"), ps[:, :],
                    qT_hi[:, :, :].rearrange("p h n -> p (h n)")).then_inc(s_qTlo, 1)

            def subtract_turns(cols, part):
                link(v_.scalar_tensor_tensor(ang[:, cols], turns(cols), -part, ang[:, cols], ALU.mult, ALU.add))

            def clamp(cols):
                v_.tensor_scalar(ang[:, cols], ang[:, cols], PI_F32, -PI_F32, ALU.min, ALU.max).then_inc(s_ang, 1)

            dve.wait_ge(s_pos, 32)
            v_.tensor_copy(pos_f[:, :], pos_i[:, :]).then_inc(s_posf, 1)
            dve.wait_ge(s_posf, 1)
            angles(v_, link, first_trig)
            link(v_.tensor_scalar(turns(first_trig), turns(first_trig), MAGIC, None, ALU.subtract))
            for part in TWO_PI:
                subtract_turns(first_trig, part)
            clamp(first_trig)
            ln1(0)
            dve.wait_ge(s_bn, KV)
            ln1_moments(0)
            dve.wait_ge(s_chi, KV)
            low(cT_lo[:, :, :], ctx_raw[:, :, :], cT_hi[:, :, :]).then_inc(s_clo, KV)
            ln1_apply(0)
            split_w(wK, 1)
            x_low(0, 0)
            dve.wait_ge(s_turns, 1)
            subtract_turns(later_trig, TWO_PI[0])
            dve.wait_ge(s_ktab, KV)
            k_products(0, 0, 0)
            dve.wait_ge(s_kprod, 2)
            rotate(v_, krot, kcos, ksin).then_inc(s_kadd, 2)
            dve.wait_ge(s_kadd, 2)
            k_products(0, 0, 1, ps_s[0])
            ln1(KV)
            split_w(wV, 3)
            dve.wait_ge(s_bn, 2 * KV)
            ln1_moments(KV)
            dve.wait_ge(s_qtab, KV)
            q_products(0, 0)
            dve.wait_ge(s_kprod, 4)
            dve.wait_ge(s_kn, 2)
            rotate(v_, krot, kcos, ksin).then_inc(s_kadd, 2)
            dve.wait_ge(s_qprod, 1)
            rotate(v_, qrot, qcos, qsin).then_inc(s_qrot, 1)
            subtract_turns(later_trig, TWO_PI[1])
            subtract_turns(later_trig, TWO_PI[2])
            clamp(later_trig)
            k_low(2, 0, 0)
            k_low(4, 0, 1, ps_o)
            q_low(0, ps_pT[1])
            v_low(0, 0, 0)
            v_low(0, 0, 1, ps_pT[0])

            def slot(g, n):
                s, b, p = flags(n)
                if s == 3 and 1 <= b <= B:
                    dve.wait_ge(s_h, g - s)
                    v_.tensor_reduce(lmax[:, 0:1], ps_kv[:, 0:NE], AX.X, ALU.max, negate=True).then_inc(s_lmax, KV)
                if n < GROUPS:
                    for t in range(2):
                        dve.wait_ge(s_score[t], g + 1)
                        v_.tensor_reduce(smax[:, 2 * t:2 * t + 2],
                                         ps_s[t][:, :].rearrange("p (h n) -> p h n", h=2),
                                         AX.X, ALU.max, negate=True).then_inc(s_max[t], 1)
                    dve.wait_ge(s_qscale, g + 1)
                    for t in range(2):
                        dve.wait_ge(s_max[t], g + 1)
                        pair = slice(2 * t, 2 * t + 2)
                        v_.tensor_tensor(sbias[:, pair], smax[:, pair], qscale[:, pair],
                                         ALU.mult).then_inc(s_bias[t], 1)
                if s == 1 and b + 1 < B:
                    x_low(g - s + KV, 1 - p)
                gating = s == 3 and 1 <= b <= B
                if gating:
                    silu(g - s)
                    gate_step(g - s, 0)
                if s == 2 and b + 2 < B:
                    ln1(g - s + 2 * KV)
                if n + 1 < GROUPS:
                    if s == 3:
                        dve.wait_ge(s_qtab, g - s + 2 * KV)
                    if s == 2 and b + 2 < B:
                        dve.wait_ge(s_bn, g - s + 3 * KV)
                    q_products(g + 1, p if s < 3 else 1 - p)
                if s == 2 and b + 2 < B:
                    ln1_moments(g - s + 2 * KV)
                if gating:
                    gate_step(g - s, 1)
                if n < GROUPS:
                    reciprocals(g, 0)
                if s == 1 and 1 <= b <= B:
                    dve.wait_ge(s_xres, (g - s) * 4)
                    dve.wait_ge(s_wo, g - s)
                    if b > 1:
                        dve.wait_ge(s_out, g - s - KV)
                    v_.tensor_tensor(x2[:, :], ps_o[:, 0:D], x_res[:, :], ALU.add).then_inc(s_x2, KV)
                if n < GROUPS:
                    dve.wait_ge(s_rec[0], g + 1)
                    for h in range(2):
                        ins = v_.tensor_scalar(probs[:, h, :], probs[:, h, :], rsums[:, h:h + 1], None, ALU.mult)
                    ins.then_inc(s_pn_dve, 1)
                if s == 1 and 1 <= b <= B:
                    dve.wait_ge(s_x2, g - s)
                    v_.bn_stats(bn6[:, 1, :], x2[:, :]).then_inc(s_bn2, KV)
                if gating:
                    gate_step(g - s, 2)
                if early_att(n):
                    att_low(g)
                if n < GROUPS:
                    if s == 1 and b > 0:
                        dve.wait_ge(s_bn2, g - s)
                    reciprocals(g, 1)
                if gating:
                    gate_step(g - s, 3)
                if s == 0 and b + 1 < B:
                    ln1_apply(g + KV)
                if s in (2, 3) and b + 1 < B:
                    k_low(g - s + KV + 2 * (s - 1), 1 - p, s - 2)
                if n == GROUPS:
                    add_experts(g, b)
                if 1 <= n <= GROUPS and not early_att(n):
                    att_low(g)
                if s == 1 and 1 <= b <= B:
                    if n > GROUPS:
                        dve.wait_ge(s_bn2, g - s)
                    v_.bn_aggr(mv[:, 1, :], bn6[:, 1, :]).then_inc(s_mv2, KV)
                if gating:
                    gate_step(g - s, 4)
                if s < 2 and b + 1 < B:
                    if s == 0:
                        dve.wait_ge(s_ktab, g + 2 * KV)
                    else:
                        dve.wait_ge(s_kadd, g - s + KV + 2)
                    k_products(g - s + KV, 1 - p, s)
                if n == 0:
                    split_w(wO, 6)
                if s == 2 and b + 1 < B:
                    v_low(g - s + KV, 1 - p, 0)
                if gating:
                    gate_step(g - s, 5)
                if n + 1 < GROUPS:
                    q_low(g + 1)
                if gating:
                    gate_step(g - s, 6)
                if s == 1 and 1 <= b <= B:
                    dve.wait_ge(s_rstd2, g - s)
                    v_.tensor_scalar(xn2[:, :], x2[:, :], mv[:, 1, 0:1], rstd[:, 1:2],
                                     ALU.subtract, ALU.mult).then_inc(s_xn2, KV)
                if n < GROUPS:
                    p_low(g, 0)
                if s == 3 and b + 1 < B:
                    v_low(g - s + KV, 1 - p, 1)
                if s == 0 and 2 <= b <= B + 1 and n != GROUPS:
                    add_experts(g, b)
                if n in w_dve:
                    split_w(*w_dve[n])
                if n < GROUPS:
                    p_low(g, 1)

            def att_low(g):
                dve.wait_ge(s_ahi, g)
                low(aT_lo[:, :, :].rearrange("p h n -> p (h n)"), ps_att[:, :],
                    aT_hi[:, :, :].rearrange("p h n -> p (h n)")).then_inc(s_alo, 1)

            def add_experts(g, b):
                dve.wait_ge(s_y, g - KV)
                if b > 2:
                    dve.wait_ge(s_store, (g - 2 * KV) * 4)
                v_.tensor_tensor(x_out[:, :], ps_q[:, 0:D], x2[:, :], ALU.add).then_inc(s_out, KV)

            def p_low(g, j):
                dve.wait_ge(s_pThi[j], g + 1)
                low(pT_lo[:, :, pair_cols(j)], ps_pT[j][:, :].rearrange("p (t n) -> p t n", t=2),
                    pT_hi[:, :, pair_cols(j)]).then_inc(s_pTlo[j], 1)

            def reciprocals(g, pair):
                dve.wait_ge(s_exp[pair], g + 1)
                heads = slice(2 * pair, 2 * pair + 2)
                v_.reciprocal(rsums[:, heads], psums[:, heads]).then_inc(s_rec[pair], 1)

            def silu(g):
                dve.wait_ge(s_lact, g)
                v_.scalar_tensor_tensor(silu2[:, :, :].rearrange("p e i -> p (e i)"),
                                        htanh[:, :, :].rearrange("p e i -> p (e i)"), 1.0,
                                        ps_kv[:, NE:NE + EI], ALU.add, ALU.mult).then_inc(s_silu, KV)

            def gate_step(g, step):
                mine = lexp[:, :].unsqueeze(2).to_broadcast([P, NE, NE])
                other = lexp[:, :].unsqueeze(1).to_broadcast([P, NE, NE])
                if step > 0:
                    dve.wait_ge(s_f, (g - KV) * 2 + (2 * KV if step == 6 else step))
                if step == 0:
                    v_.tensor_tensor(beats[:, :, :], other, mine, ALU.is_gt)
                    v_.tensor_tensor(ties[:, :, :], other, mine, ALU.is_equal).then_inc(s_f, 1)
                if step == 1:
                    v_.tensor_tensor(ties[:, :, :], ties[:, :, :], earlier[:, :, :], ALU.mult)
                    v_.reciprocal(lrec[:, :], lsum[:, :]).then_inc(s_f, 1)
                if step == 2:
                    v_.tensor_tensor(beats[:, :, :], beats[:, :, :], ties[:, :, :], ALU.add).then_inc(s_f, 1)
                if step == 3:
                    v_.tensor_reduce(rank[:, :], beats[:, :, :], AX.X, ALU.add).then_inc(s_f, 1)
                if step == 4:
                    v_.scalar_tensor_tensor(gate[:, :], rank[:, :], 1.5, lexp[:, :],
                                            ALU.is_lt, ALU.mult).then_inc(s_f, 1)
                if step == 5:
                    v_.tensor_scalar(gate_n[:, :], gate[:, :], lrec[:, 0:1], 0.5,
                                     ALU.mult, ALU.mult).then_inc(s_f, 2 * KV - 5)
                if step == 6:
                    v_.tensor_tensor(act_g[:, :, :], silu2[:, :, :],
                                     gate_n[:, :].unsqueeze(2).to_broadcast([P, NE, NI]), ALU.mult).then_inc(s_gate, KV)

            run_slots(dve, slot)

        @block.tensor
        def _(pe):
            t_ = nc.tensor

            def three(out, l_hi, l_lo, r_hi, r_lo, first, last):
                t_.matmul(out, l_hi, r_lo, start=first, stop=False)
                t_.matmul(out, l_lo, r_hi, start=False, stop=False)
                return t_.matmul(out, l_hi, r_hi, start=False, stop=last)

            def flip(out, src):
                return t_.matmul(out, src, ident[:, :], is_transpose=True, start=True, stop=True)

            def keep_busy(flips, ps):
                with pe.Fori(0, flips // 4):
                    for _ in range(4):
                        flip(ps[:, 0:P], ident[:, :])

            def project(ps, l_hi, l_lo, c):
                for t in range(DT):
                    cols = slice(t * GRP, (t + 1) * GRP)
                    ins = three(ps[:, :], l_hi[:, t, :], l_lo[:, t, :], w_hi[:, c, cols], w_lo[:, c, cols],
                                t == 0, t == DT - 1)
                return ins

            def x_flip(g):
                pe.wait_ge(s_xn, g + KV)
                for t in range(DT):
                    ins = flip(ps_tr[:, t * P:(t + 1) * P], xn[:, t * P:(t + 1) * P])
                ins.then_inc(s_xTps, KV)

            def queries(g, p, s):
                after(pe, s_qsq, g)
                project(ps_q, xT_hi[p], xT_lo[p], wQ + s).then_inc(s_qps, 1)

            def kv_unit(g, p, u, ps=ps_kv):
                if u == 0:
                    pe.wait_ge(s_chi, g + KV)
                    pe.wait_ge(s_clo, g + KV)
                if u == 1:
                    pe.wait_ge(s_xTlo, g + KV)
                l_hi, l_lo = (cT_hi, cT_lo) if u % 2 == 0 else (xT_hi[p], xT_lo[p])
                project(ps, l_hi, l_lo, wK if u < 2 else wV).then_inc(s_kvps, 1)

            def k_flip(u, ps=ps_tr):
                pe.wait_ge(s_kn, u)
                for h in range(KV):
                    ins = flip(ps[:, h * P:(h + 1) * P], krot_n[:, h, :])
                ins.then_inc(s_kTps, 2)

            def q_flip(g, ps=ps_tr):
                pe.wait_ge(s_qrot, g + 1)
                for h in range(REP):
                    ins = flip(ps[:, h * P:(h + 1) * P], qrot[:, h, :])
                ins.then_inc(s_qTps, 1)

            def scores(g, p, s):
                pe.wait_ge(s_qTlo, g + 1)
                for h in range(REP):
                    if h % 2 == 0:
                        after(pe, s_exp[h // 2], g)
                    ins = three(ps_s[h // 2][:, (h % 2) * KEYS:(h % 2 + 1) * KEYS], qT_hi[:, h, :], qT_lo[:, h, :],
                                kT_hi[p][:, s, :], kT_lo[p][:, s, :], True, True)
                    if h % 2:
                        ins.then_inc(s_score[h // 2], 1)

            def p_flip(g, j):
                pe.wait_ge((s_pn_dve, s_pn_pool)[j], g + 1)
                for t in range(2):
                    for h in range(2):
                        at = (2 * t + h) * P
                        ins = flip(ps_pT[j][:, at:at + P], probs[:, 2 * j + h, t * P:(t + 1) * P])
                ins.then_inc(s_pTps[j], 1)

            def values(g, p, s):
                cols = slice(s * HD, (s + 1) * HD)
                pe.wait_ge(s_pTlo[1], g + 1)
                pe.wait_ge(s_pTlo[0], g + 1)
                for t in range(2):
                    ins = three(ps_att[:, :], v_hi[p][:, t, cols], v_lo[p][:, t, cols], pT_hi[:, t, :],
                                pT_lo[:, t, :], t == 0, t == 1)
                ins.then_inc(s_att, 1)

            def gated_flip(g):
                pe.wait_ge(s_gate, g - KV)
                flip(ps_tr[:, 0:P], act_g[:, :, :].rearrange("p e i -> p (e i)")).then_inc(s_agTps, KV)

            def experts_out(g):
                pe.wait_ge(s_agT, g - KV)
                t_.matmul(ps_q[:, 0:D], agT[:, :], up_w[:, :], start=True, stop=True).then_inc(s_y, KV)

            def output(g, s):
                pe.wait_ge(s_alo, g + 1)
                for h in range(REP):
                    cols = slice(h * D, (h + 1) * D)
                    ins = three(ps_o[:, 0:D], aT_hi[:, h, :], aT_lo[:, h, :], w_hi[:, wO + s, cols],
                                w_lo[:, wO + s, cols], s == 0 and h == 0, s == KV - 1 and h == REP - 1)
                ins.then_inc(s_wo, 1)

            pe.wait_ge(s_const, 4)
            keep_busy(28, ps_tr)
            x_flip(0)
            pe.wait_ge(s_wlo_dve, 1)
            kv_unit(0, 0, 0)
            kv_unit(0, 0, 1, ps_s[0])
            pe.wait_ge(s_wlo_pool, 1)
            queries(0, 0, 0)
            pe.wait_ge(s_wlo_dve, 2)
            pe.wait_ge(s_ksq, 2)
            kv_unit(0, 0, 2)
            k_flip(2)
            kv_unit(0, 0, 3, ps_pT[0])
            q_flip(0, ps_pT[1])
            k_flip(4, ps_o)
            keep_busy(16, ps_s[1])
            pe.wait_ge(s_ksq, 4)

            def slot(g, n):
                s, b, p = flags(n)
                nxt = b + 1 < B
                if n < GROUPS:
                    if s == 0:
                        pe.wait_ge(s_kTlo, g + KV)
                    scores(g, p, s)
                if s == 2 and 1 <= b <= B:
                    if n > GROUPS:
                        pe.wait_ge(s_agT, g - s - KV)
                        keep_busy(28, ps_tr)
                    pe.wait_ge(s_xn2, g - s)
                    for t in range(DT):
                        ins = flip(ps_tr[:, t * P:(t + 1) * P], xn2[:, t * P:(t + 1) * P])
                    ins.then_inc(s_x2Tps, KV)
                if n + 1 < GROUPS:
                    if n == 0:
                        pe.wait_ge(s_wlo_pool, 2)
                    elif n < 3:
                        pe.wait_ge(s_wlo_dve, n + 3)
                    if s == 1 and b >= 2:
                        pe.wait_ge(s_out, g - s - KV)
                    queries(g + 1, p if s < 3 else 1 - p, (s + 1) % KV)
                if n == GROUPS:
                    gated_flip(g)
                    experts_out(g)
                if 1 <= n <= GROUPS:
                    if s == 1:
                        pe.wait_ge(s_vlo, g - s + KV)
                    values(g - 1, p if s > 0 else 1 - p, (s - 1) % KV)
                if s in (2, 3) and nxt:
                    if s == 2 and b > 0:
                        pe.wait_ge(s_x2T, g - s)
                    k_flip(g - s + KV + 2 * (s - 1))
                if n == TAIL_TO - 1:
                    keep_busy(32, ps_tr)
                if s == 0 and 2 <= b <= B + 1 and n != GROUPS:
                    gated_flip(g)
                if nxt:
                    if s == 0:
                        pe.wait_ge(s_vlo, g + KV)
                    if s == 1:
                        pe.wait_ge(s_ksq, g - s + KV + 2)
                    if s == 2:
                        pe.wait_ge(s_ksq, g - s + 2 * KV)
                    if s == 3:
                        pe.wait_ge(s_vlo, g - s + KV + 2)
                        after(pe, s_silu, g - s)
                    kv_unit(g - s + KV, 1 - p, s)
                if n == GROUPS - 1:
                    keep_busy(16, ps_tr)
                if n < GROUPS:
                    p_flip(g, 0)
                if n == GROUPS - 1:
                    pe.wait_ge(s_alo, g)
                    p_flip(g, 1)
                if n + 1 < GROUPS:
                    if s in (2, 3) and nxt:
                        pe.wait_ge(s_kTlo, g - s + KV + 2 * (s - 1))
                    elif s == 1 and nxt:
                        pe.wait_ge(s_xTlo, g - s + 2 * KV)
                    elif s == 0 and b > 1:
                        pe.wait_ge(s_agT, g - KV)
                    elif s == 2:
                        pe.wait_ge(s_x2T, g - s)
                    q_flip(g + 1)
                if 1 <= n <= GROUPS:
                    if s == 1 and b > 0:
                        pe.wait_ge(s_x2, g - s)
                    if n == 1:
                        pe.wait_ge(s_wlo_dve, 3)
                    elif n <= KV:
                        pe.wait_ge(s_wlo_pool, n + 1)
                    if n == GROUPS:
                        keep_busy(12, ps_tr)
                    output(g - 1, (s - 1) % KV)
                if s == 0 and 2 <= b <= B + 1 and n != GROUPS:
                    if n + 1 < GROUPS:
                        pe.wait_ge(s_qsq, g + 2)
                    experts_out(g)
                if n < GROUPS - 1:
                    p_flip(g, 1)
                if s == 0 and nxt:
                    pe.wait_ge(s_qTlo, g + 2)
                    x_flip(g + KV)
                if s == 2 and 1 <= b <= B:
                    if nxt:
                        pe.wait_ge(s_vlo, g - s + KV + 2)
                    else:
                        pe.wait_ge(s_silu, g - s - KV)
                    if b == 1:
                        pe.wait_ge(s_small, 32)
                    pe.wait_ge(s_x2T, g - s)
                    for t in range(DT):
                        ins = t_.matmul(ps_kv[:, 0:NE + EI], x2T[:, t, :], ffn_in_w[:, t, :],
                                        start=t == 0, stop=t == DT - 1)
                    ins.then_inc(s_h, KV)

            run_slots(pe, slot)


def kernel(**inputs):
    import concourse.bacc as bacc
    import numpy as np
    from concourse.bass_utils import run_bass_kernel_spmd

    def arr(name):
        return np.asarray(inputs[name])

    def heads_in(w):
        return w.reshape(-1, GRP, DT, P).transpose(0, 3, 2, 1).reshape(-1, P, CH)

    wo = arr("L0_xattn_Wo").reshape(D, KV, REP, HD).transpose(1, 3, 2, 0).reshape(KV, P, CH)
    weights = np.concatenate([heads_in(arr("L0_xattn_Wk")), heads_in(arr("L0_xattn_Wv")),
                              heads_in(arr("L0_xattn_Wq")), wo])
    positions = np.stack([arr("pos_BxS2"), arr("itok_BxS_4096_4607")], axis=1).reshape(2 * B, S).T
    experts_in = np.concatenate([arr("L0_ffn_router_w"), arr("L0_ffn_down_w").reshape(EI, D)])
    freq = (np.float32(1.0) / np.float32(10000.0) ** (np.arange(0, HD, 2, dtype=np.float32) / np.float32(HD)))
    data = {
        "x": arr("x"),
        "ctxT": arr("ctx_2048").reshape(B, S, DT, P).transpose(0, 3, 2, 1).reshape(B, P, DT * S),
        "positions": positions,
        "weights": weights,
        "norms": np.concatenate([arr("L0_xattn_q_norm_w"), arr("L0_xattn_k_norm_w")]),
        "experts_in": experts_in.reshape(NE + EI, DT, P).transpose(2, 1, 0),
        "experts_out": arr("L0_ffn_up_w").transpose(0, 2, 1).reshape(EI, D),
        "frequencies": freq.astype(np.float32),
    }
    data = {name: np.ascontiguousarray(a) for name, a in data.items()}
    nc = bacc.Bacc("TRN2", target_bir_lowering=False, num_devices=1)
    args = [nc.dram_tensor(f"in_{name}", a.shape, mybir.dt.from_np(a.dtype), kind="ExternalInput").ap()
            for name, a in data.items()]
    args.append(nc.dram_tensor("out", (B, S, D), F32, kind="ExternalOutput").ap())
    xattn_ffn(nc, *args)
    result = run_bass_kernel_spmd(nc, [{f"in_{name}": a for name, a in data.items()}], core_ids=[0])
    return result.results[0]["out"]
```
